# Optimizing a Trainium2 kernel written in Bass

```python
import numpy as np
import jax
import jax.numpy as jnp

def _softmax(x, axis=-1):
    return jax.nn.softmax(x, axis=axis)

def _gelu(x):
    return jax.nn.gelu(x, approximate=True)

def _silu(x):
    return jax.nn.silu(x)

def _sigmoid(x):
    return jax.nn.sigmoid(x)

def _layernorm(x, axis=-1, eps=1e-05):
    m = jnp.mean(x, axis=axis, keepdims=True)
    v = jnp.var(x, axis=axis, keepdims=True)
    return (x - m) / jnp.sqrt(v + eps)

def _scatter_add(tgt, idx, src, axis=0):
    return tgt.at[idx].add(src)

def _segment_sum(src, seg, n):
    return jax.ops.segment_sum(src, seg, n)
kernel_name = 'mk_adaln_ffn_d1_seqx_r4_bf0c65'

def setup_inputs(seed: int=0):
    np.random.seed(seed)
    _w = jnp.asarray

    def _rec_inputs():
        import jax
        import jax.numpy as jnp
        _rk = jax.random.key(seed)
        x = -0.000125 + 0.9999 * jax.random.normal(jax.random.fold_in(_rk, 1), (32, 64, 1024), jnp.float32)
        _lenS = 64 - jax.random.randint(jax.random.fold_in(_rk, 7), (32,), 0, max(1, 64 // 4) + 1, jnp.int32)
        _lenS2 = 64 - jax.random.randint(jax.random.fold_in(_rk, 8), (32,), 0, max(1, 64 // 4) + 1, jnp.int32)
        cond_128 = 0.0061147 + 1.02565 * jax.random.normal(jax.random.fold_in(_rk, 11), (32, 128), jnp.float32)
        fside_S_0 = -0.022604 + 0.987366 * jax.random.normal(jax.random.fold_in(_rk, 12), (64,), jnp.float32)
        return (x, cond_128, fside_S_0)
    x, cond_128, fside_S_0 = _rec_inputs()

    def _L0_cond_setup():
        import jax, jax.numpy as jnp
        import numpy as np
        from jax import lax
        N, C_IN, L = (32, 64, 1024)
        C_OUT, K, GROUPS = (64, 9, 4)
        C_DIM, PAD, STRIDE = (128, 4, 1)
        key = jax.random.key(seed)
        k1, k2, k3, k4, k5 = jax.random.split(key, 5)
        x = jax.random.normal(k1, (N, C_IN, L), dtype=jnp.float32)
        c = jax.random.normal(k2, (N, C_DIM), dtype=jnp.float32)
        weight = jax.random.normal(k3, (C_OUT, C_IN // GROUPS, K), dtype=jnp.float32)
        c_weight = jax.random.normal(k4, (C_OUT, C_DIM), dtype=jnp.float32)
        bias = jax.random.normal(k5, (C_OUT,), dtype=jnp.float32)
        return {'x': x, 'c': c, 'weight': weight, 'c_weight': c_weight, 'bias': bias}
    _L0_cond_all = _L0_cond_setup()
    _L0_cond_in = {k: v for k, v in _L0_cond_all.items() if k in ('weight', 'c_weight')}
    del _L0_cond_all

    def _L0_ffn_setup():
        import jax, jax.numpy as jnp
        import numpy as np
        IN_F = 1024
        OUT_F = 1024
        RANK = 8
        NUM_EXPERTS = 64
        TOP_K = 16
        ROUTER_DIM = 16
        ALPHA = 32
        SCALING = ALPHA / TOP_K
        BOTTLENECK = NUM_EXPERTS * RANK
        key = jax.random.key(seed)
        ks = jax.random.split(key, 5)
        x = jax.random.normal(ks[0], (4, 1024, IN_F), dtype=jnp.float32)
        bound_a = float(np.sqrt(6.0 / IN_F))
        A_w = jax.random.uniform(ks[1], (BOTTLENECK, IN_F), jnp.float32, -bound_a, bound_a)
        B_w = jax.random.normal(ks[2], (OUT_F, BOTTLENECK), dtype=jnp.float32) * 0.02
        Wq_w = jax.random.normal(ks[3], (ROUTER_DIM, IN_F), dtype=jnp.float32) * 0.02
        keys = jax.random.normal(ks[4], (NUM_EXPERTS, ROUTER_DIM), dtype=jnp.float32) * 0.01
        return {'x': x, 'A_w': A_w, 'B_w': B_w, 'Wq_w': Wq_w, 'keys': keys}
    _L0_ffn_all = _L0_ffn_setup()
    _L0_ffn_in = {k: v for k, v in _L0_ffn_all.items() if k in ('A_w', 'B_w', 'Wq_w', 'keys')}
    del _L0_ffn_all
    return {'x': x, 'cond_128': cond_128, 'fside_S_0': fside_S_0, 'L0_cond_weight': _L0_cond_in['weight'], 'L0_cond_c_weight': _L0_cond_in['c_weight'], 'L0_ffn_A_w': _L0_ffn_in['A_w'], 'L0_ffn_B_w': _L0_ffn_in['B_w'], 'L0_ffn_Wq_w': _L0_ffn_in['Wq_w'], 'L0_ffn_keys': _L0_ffn_in['keys']}

def reference(x, cond_128, fside_S_0, L0_cond_weight, L0_cond_c_weight, L0_ffn_A_w, L0_ffn_B_w, L0_ffn_Wq_w, L0_ffn_keys):
    import jax
    import jax.numpy as jnp

    def _L0_cond_ref(x, c, weight, c_weight, bias):
        import jax, jax.numpy as jnp
        import numpy as np
        from jax import lax
        N, C_IN, L = (32, 64, 1024)
        C_OUT, K, GROUPS = (64, 9, 4)
        C_DIM, PAD, STRIDE = (128, 4, 1)
        out = lax.conv_general_dilated(x, weight, window_strides=(STRIDE,), padding=[(PAD, PAD)], dimension_numbers=('NCH', 'OIH', 'NCH'), feature_group_count=GROUPS)
        ctx = jnp.einsum('nd,od->no', c, c_weight)
        out = out + ctx[:, :, None] + bias[None, :, None]
        return out

    def _L0_ffn_ref(x, A_w, B_w, Wq_w, keys):
        import jax, jax.numpy as jnp
        import numpy as np
        IN_F = 1024
        OUT_F = 1024
        RANK = 8
        NUM_EXPERTS = 64
        TOP_K = 16
        ROUTER_DIM = 16
        ALPHA = 32
        SCALING = ALPHA / TOP_K
        BOTTLENECK = NUM_EXPERTS * RANK
        q = jnp.einsum('bsd,rd->bsr', x, Wq_w)
        scores = jnp.einsum('bsr,er->bse', q, keys)
        top_vals, top_idx = jax.lax.top_k(scores, TOP_K)
        top_w = jax.nn.softmax(top_vals, axis=-1)
        gate = jnp.sum(jax.nn.one_hot(top_idx, NUM_EXPERTS, dtype=top_w.dtype) * top_w[..., None], axis=-2)
        z = jnp.einsum('bsd,nd->bsn', x, A_w)
        z = z.reshape(*z.shape[:-1], NUM_EXPERTS, RANK)
        z_gated = (z * gate[..., None]).reshape(*z.shape[:-2], BOTTLENECK)
        out = jnp.einsum('bsn,on->bso', z_gated, B_w) * SCALING
        return out
    x = x + _L0_ffn_ref(_L0_cond_ref(x, cond_128, L0_cond_weight, L0_cond_c_weight, fside_S_0), L0_ffn_A_w, L0_ffn_B_w, L0_ffn_Wq_w, L0_ffn_keys)
    return x

_drawn_inputs = setup_inputs


def setup_inputs(seed=0):
    import zlib

    import numpy as np

    out = dict(_drawn_inputs(seed))
    spreads = {}
    factors = {}
    for name, (base, spread) in spreads.items():
        noise = np.random.default_rng([zlib.crc32(name.encode()), seed]).standard_normal(out[name].shape)
        drawn = base * np.exp(spread * noise) if base else spread * noise
        out[name] = jnp.asarray(drawn.astype(out[name].dtype))
    for name, factor in factors.items():
        out[name] = (out[name] * factor).astype(out[name].dtype)
    return out
```

```python
from contextlib import ExitStack

import concourse.bass as bass
from concourse import mybir

ALU = mybir.AluOpType
ACT = mybir.ActivationFunctionType
F32 = mybir.dt.float32
F32R = mybir.dt.float32r

P = 128
TAKEN = -float(2**127)
SCALING = 2.0


def adaln_ffn(nc, x, cond, bias, conv_w, cond_w, A_w, B_w, Wq_w, keys, out):
    N, C, L = x.shape
    CO, CI, K = conv_w.shape
    G = C // CI
    PAD = K // 2
    R = 8
    NB = L // R
    NM = NB + 1
    LP = R * NM
    NT = N * C // P
    NN = P // C
    NG = NN * G
    J = A_w.shape[0]
    E, RD = keys.shape
    RANK = J // E
    JC = J // P
    JQ = J + RD
    HB = JQ // 2
    OC = L // P
    D = cond.shape[1]
    assert CI * R == P and NB == P and D == P and K <= R + 1 and C == 64 and NN == 2
    assert 2 * HB == JQ and HB <= 512 and HB % RANK == 0 and NT == 16

    x_v = x.rearrange("(i n) c l -> i (n c) l", n=NN)
    out_v = out.rearrange("(i n) c l -> i (n c) l", n=NN)

    with ExitStack() as ctx:
        def sb(name, shape, dt=F32):
            return ctx.enter_context(nc.sbuf_tensor(name, shape, dt))

        def ps(name, shape):
            return ctx.enter_context(nc.psum_tensor(name, shape, F32))

        def sem(name):
            return ctx.enter_context(nc.semaphore(name))

        ident = sb("ident", [P, P])
        ones = sb("ones", [P, P])
        x_all = sb("x_all", [P, NT, LP])
        x_cut = sb("x_cut", [P, R, NM])
        x_blk = sb("x_blk", [P, NG, NM])
        x_hi = sb("x_hi", [P, NG, NM], F32R)
        x_lo = sb("x_lo", [P, NG, NM], F32R)
        w_pad = sb("w_pad", [CO, CI, 3 * R])
        w_cut = sb("w_cut", [CO, 2, R, P])
        w_hi = sb("w_hi", [P, 2, G, R * CI], F32R)
        w_lo = sb("w_lo", [P, 2, G, R * CI], F32R)
        h_hi = sb("h_hi", [P, R, P], F32R)
        h_lo = sb("h_lo", [P, R, P], F32R)
        a_hi = sb("a_hi", [P, R, JQ], F32R)
        a_lo = sb("a_lo", [P, R, JQ], F32R)
        b_hi = sb("b_hi", [P, JC, L], F32R)
        b_lo = sb("b_lo", [P, JC, L], F32R)
        wq_nat = sb("wq_nat", [RD, L])
        keys_nat = sb("keys_nat", [E, RD])
        keys_t = sb("keys_t", [RD, E])
        cw_nat = sb("cw_nat", [P, D])
        cw_t = sb("cw_t", [D, P])
        c_nat = sb("c_nat", [N, D])
        c_t = sb("c_t", [D, N])
        bias2 = sb("bias2", [P, 1])
        u = sb("u", [P, NT])
        row_sum = sb("row_sum", [P, JC + 1])
        diag = sb("diag", [P, JQ])
        sum_bc = sb("sum_bc", [P, JQ])
        z_s = sb("z_s", [P, J])
        z_g = sb("z_g", [P, J])
        zt_hi = sb("zt_hi", [P, JC, P], F32R)
        zt_lo = sb("zt_lo", [P, JC, P], F32R)
        q_s = sb("q_s", [P, RD])
        q_t = sb("q_t", [RD, P])
        sc = sb("sc", [P, E])
        sc_a = sb("sc_a", [P, E])
        sc_b = sb("sc_b", [P, E])
        top_a = sb("top_a", [P, 8])
        top_b = sb("top_b", [P, 8])
        neg_max = sb("neg_max", [P, 1])
        e_all = sb("e_all", [P, E])
        e_top = sb("e_top", [P, E])
        e_sum = sb("e_sum", [P, 1])
        e_inv = sb("e_inv", [P, 1])
        o_sb = sb("o_sb", [P, L])

        A_AT, B_AT = NT - 2 * JC, NT - JC
        a_nat = x_all[:, A_AT:A_AT + JC, PAD:PAD + L]
        b_nat = x_all[:, B_AT:NT, PAD:PAD + L]

        p_conv = ps("p_conv", [P, 2, 512])
        p_z = ps("p_z", [P, 2, 512])
        p_out = ps("p_out", [P, 2, 512])
        p_t = ps("p_t", [P, 512])
        p_s = ps("p_s", [P, 512])
        QT, SC, KT, CT, CWT, U = (slice(a, a + n) for a, n in
                                  ((0, P), (128, E), (192, E), (256, N), (288, P), (416, N)))

        def a_bank(r):
            return (p_t[:], p_z[:, 0, :], p_z[:, 1, :])[r % 3]

        s_const = sem("s_const")
        s_iz = sem("s_iz")
        s_pads = sem("s_pads")
        s_wz = sem("s_wz")
        s_w = sem("s_w")
        s_small = [sem(f"s_small{k}") for k in range(6)]
        s_a = [sem(f"s_a{k}") for k in range(JC)]
        s_b = [sem(f"s_b{k}") for k in range(JC)]
        s_x0 = [sem(f"s_x0{k}") for k in range(4)]
        s_x = sem("s_x")
        s_cut = sem("s_cut")
        s_blk = sem("s_blk")
        s_xhi = sem("s_xhi")
        s_xlo = sem("s_xlo")
        s_wt = sem("s_wt")
        s_wc = sem("s_wc")
        s_whi = sem("s_whi")
        s_wlo = sem("s_wlo")
        s_st = sem("s_st")
        s_sc = sem("s_sc")
        s_up = sem("s_up")
        s_u = sem("s_u")
        s_at = sem("s_at")
        s_ahi = sem("s_ahi")
        s_alo = sem("s_alo")
        s_rs = sem("s_rs")
        s_dg = sem("s_dg")
        s_bcp = sem("s_bcp")
        s_bc = sem("s_bc")
        s_bt = sem("s_bt")
        s_bhi = sem("s_bhi")
        s_blo = sem("s_blo")
        s_conv = sem("s_conv")
        s_hhi = sem("s_hhi")
        s_hlo = sem("s_hlo")
        s_zq = sem("s_zq")
        s_z = sem("s_z")
        s_zs = sem("s_zs")
        s_q = sem("s_q")
        s_qtp = sem("s_qtp")
        s_qt = sem("s_qt")
        s_scp = sem("s_scp")
        s_nm = sem("s_nm")
        s_e = sem("s_e")
        s_dve = sem("s_dve")
        s_alone = sem("s_alone")
        s_zg = sem("s_zg")
        s_ztp = sem("s_ztp")
        s_zthi = sem("s_zthi")
        s_ztlo = sem("s_ztlo")
        s_out = sem("s_out")
        s_osb = sem("s_osb")
        s_stored = sem("s_stored")

        block = ctx.enter_context(nc.Block())

        def real(t):
            return not isinstance(t, int) or 0 <= t < NT

        def after(eng, s, count):
            if not isinstance(count, int) or count > 0:
                eng.wait_ge(s, count)

        def cut_w(engine, s):
            for r in range(R):
                at = R * s - r + R
                cut = engine.tensor_copy(w_cut[:, s, r, :].rearrange("o (c p) -> o c p", p=R), w_pad[:, :, at:at + R])
            cut.then_inc(s_wc, 1)

        def relayout(eng, t):
            eng.wait_ge(s_cut, t + 1)
            after(eng, s_xhi, t)
            after(eng, s_xlo, t)
            for k in range(NG):
                eng.dma_start(x_blk[:, k, :], x_cut[k * CI:(k + 1) * CI]).then_inc(s_blk, 16)

        @block.sync
        def _(sp):
            def load_x(t, s):
                sp.dma_start(x_all[:, t, PAD:PAD + L], x_v[t]).then_inc(s, 16)

            def body(i):
                if not isinstance(i, int):
                    sp.lower_val(i + 2)
                    sp.lower_val(i + 3)
                if real(i + 2):
                    relayout(sp, i + 2)
                if real(i + 4):
                    after(sp, s_x, 16 * i)
                    load_x(i + 4, s_x)
                if real(i - 1):
                    sp.wait_ge(s_osb, 2 * i)
                    sp.dma_start(out_v[i - 1], o_sb[:]).then_inc(s_stored, 16)

            load_x(0, s_x0[0])
            sp.wait_ge(s_wz, 1)
            sp.dma_start(w_pad[:, :, R:R + K], conv_w).then_inc(s_w, 16)
            for jc in range(JC):
                sp.dma_start(a_nat[:, jc, :], A_w[jc * P:(jc + 1) * P, :]).then_inc(s_a[jc], 16)
            load_x(1, s_x0[1])
            for k in range(JC):
                sp.dma_start(b_nat[:, k, :].rearrange("o (c j) -> o c j", c=2),
                             B_w[2 * k * P:2 * (k + 1) * P, :].rearrange("(c o) j -> o c j", c=2)).then_inc(s_b[k], 16)
            load_x(2, s_x0[2])
            load_x(3, s_x0[3])
            relayout(sp, 1)
            body(0)
            body(1)
            sp.wait_ge(s_at, R)
            sp.wait_ge(s_bt, 2 * JC)
            sp.wait_ge(s_rs, JC)
            with sp.Fori(2, NT - 4) as i:
                body(i)
            for i in range(NT - 4, NT + 1):
                body(i)
            sp.wait_ge(s_stored, 16 * NT)

        @block.gpsimd
        def _(pool):
            def cut(t):
                if isinstance(t, int) and t < 4:
                    pool.wait_ge(s_x0[t], 16)
                else:
                    pool.wait_ge(s_x, 16 * (t - 3))
                after(pool, s_blk, 16 * NG * t)
                nc.gpsimd.tensor_copy(x_cut[:], x_all[:, t, :].rearrange("c (m p) -> c p m", p=R)).then_inc(s_cut, 1)

            nc.gpsimd.memset(ident[:], 0.0).then_inc(s_iz, 1)
            nc.gpsimd.memset(ones[:], 1.0).then_inc(s_const, 1)
            pool.wait_ge(s_iz, 1)
            nc.gpsimd.affine_select(out=ident[:], in_=ident[:], compare_op=ALU.not_equal, fill=1.0, base=0,
                                    pattern=[[-1, P]], channel_multiplier=1).then_inc(s_const, 1)
            pool.wait_ge(s_w, 16)
            cut_w(nc.gpsimd, 1)
            pool.wait_ge(s_pads, 2)
            cut(0)
            cut(1)
            cut(2)
            cut(3)
            with pool.Fori(4, NT) as t:
                cut(t)

        @block.scalar
        def _(act):
            def high(dst, src, s, scale=1.0):
                nc.scalar.activation(dst, src, ACT.Copy, scale=scale).then_inc(s, 1)

            def split_x(t):
                act.wait_ge(s_blk, 16 * NG * (t + 1))
                after(act, s_conv, 2 * t)
                high(x_hi[:], x_blk[:], s_xhi)

            def split_h(t):
                for k in range(2):
                    act.wait_ge(s_conv, 2 * t + k + 1)
                    after(act, s_z, t)
                    high(h_hi[:, :, k * P // 2:(k + 1) * P // 2].rearrange("b r (g c) -> b g r c", c=CI),
                         p_conv[:, k, :].rearrange("b (g r c) -> b g r c", r=R, c=CI), s_hhi)

            def body(i):
                if real(i - 1):
                    act.wait_ge(s_ztp, i)
                    after(act, s_out, 2 * (i - 1))
                    high(zt_hi[:], p_t[:].rearrange("j (c t) -> j c t", c=JC), s_zthi)
                if real(i):
                    act.wait_ge(s_qtp, i + 1)
                    nc.scalar.activation(q_t[:], p_s[0:RD, QT], ACT.Copy).then_inc(s_qt, 1)
                    act.wait_ge(s_nm, i + 1)
                    nc.scalar.activation(e_all[:], sc[:], ACT.Exp, bias=neg_max[:]).then_inc(s_e, 1)
                if real(i + 1):
                    split_h(i + 1)
                if real(i + 2):
                    split_x(i + 2)

            for k in range(2):
                act.dma_start(cw_nat[k * CO:(k + 1) * CO, :], cond_w).then_inc(s_small[0], 16)
                act.dma_start(bias2[k * CO:(k + 1) * CO, :], bias.rearrange("(o a) -> o a", a=1)).then_inc(s_small[1], 16)
            act.dma_start(c_nat[:], cond).then_inc(s_small[2], 16)
            act.dma_start(keys_nat[:], keys).then_inc(s_small[3], 16)
            act.dma_start(wq_nat[:], Wq_w).then_inc(s_small[4], 16)
            for s in range(2):
                act.wait_ge(s_wt, s + 1)
                high(w_hi[:, s].rearrange("k g (r c) -> k r g c", c=CI),
                     p_out[:, s, :].rearrange("k (r g c) -> k r g c", g=G, c=CI), s_whi)
            relayout(act, 0)
            act.wait_ge(s_st, 3)
            nc.scalar.activation(cw_t[:], p_s[:, CWT], ACT.Copy).then_inc(s_sc, 1)
            nc.scalar.activation(c_t[:], p_s[:, CT], ACT.Copy).then_inc(s_sc, 1)
            nc.scalar.activation(keys_t[:], p_s[0:RD, KT], ACT.Copy).then_inc(s_sc, 1)
            split_x(0)
            split_h(0)
            for r in range(R):
                act.wait_ge(s_at, r + 1)
                high(a_hi[:, r, 0:J], a_bank(r), s_ahi)
            act.wait_ge(s_at, R + 1)
            high(a_hi[:, :, J:JQ], p_out[:, 0, 0:R * RD].rearrange("b (r q) -> b r q", q=RD), s_ahi)
            act.wait_ge(s_bcp, 1)
            nc.scalar.activation(sum_bc[:, 0:J], p_out[:, 1, :], ACT.Copy).then_inc(s_bc, 1)
            nc.scalar.activation(sum_bc[:, J:JQ], p_s[:, 0:RD], ACT.Copy).then_inc(s_bc, 1)
            split_x(1)
            body(0)
            for n in range(2 * JC):
                act.wait_ge(s_bt, n + 1)
                high(b_hi[:, n // 2, n % 2 * 512:(n % 2 + 1) * 512], p_out[:, n % 2, :], s_bhi, SCALING)
            body(1)
            with act.Fori(2, NT - 2) as i:
                body(i)
            for i in range(NT - 2, NT + 1):
                body(i)

        @block.tensor
        def _(pe):
            def three(dst, s_hi, s_lo, m_hi, m_lo, first, last):
                nc.tensor.matmul(dst, s_hi, m_hi, start=first, stop=False)
                nc.tensor.matmul(dst, s_hi, m_lo, start=False, stop=False)
                return nc.tensor.matmul(dst, s_lo, m_hi, start=False, stop=last)

            def conv(t):
                pe.wait_ge(s_xhi, t + 1)
                pe.wait_ge(s_xlo, t + 1)
                for k in range(2):
                    after(pe, s_hhi, 2 * t)
                    after(pe, s_hlo, 2 * t)
                    for j in range(NG // 2):
                        n = k * NG // 2 + j
                        for s in range(2):
                            mm = three(p_conv[:, k, j * P:(j + 1) * P], x_hi[:, n, s:s + NB], x_lo[:, n, s:s + NB],
                                       w_hi[:, s, n % G, :], w_lo[:, s, n % G, :], s == 0, s == 1)
                    mm.then_inc(s_conv, 1)

            def z_bank(k, phases):
                for r in phases:
                    cols = slice(k * HB, (k + 1) * HB)
                    mm = three(p_z[:, k, 0:HB], h_hi[:, r, :], h_lo[:, r, :], a_hi[:, r, cols], a_lo[:, r, cols],
                               r == 0, r == R - 1)
                return mm

            def body(i):
                if real(i - 1):
                    pe.wait_ge(s_zg, i)
                    for c in range(JC):
                        mm = nc.tensor.transpose(p_t[:, c * P:(c + 1) * P], z_g[:, c * P:(c + 1) * P], ident[:])
                    mm.then_inc(s_ztp, 1)
                if real(i):
                    pe.wait_ge(s_hhi, 2 * (i + 1))
                    pe.wait_ge(s_hlo, 2 * (i + 1))
                    z_bank(1, range(R)).then_inc(s_zq, 1)
                    z_bank(0, range(R // 2))
                    pe.wait_ge(s_q, i + 1)
                    nc.tensor.transpose(p_s[0:RD, QT], q_s[:], ident[:]).then_inc(s_qtp, 1)
                    z_bank(0, range(R // 2, R)).then_inc(s_z, 1)
                    pe.wait_ge(s_qt, i + 1)
                    nc.tensor.matmul(p_s[:, SC], q_t[:], keys_t[:], start=True, stop=True).then_inc(s_scp, 1)
                if real(i + 1):
                    conv(i + 1)
                if real(i - 1):
                    pe.wait_ge(s_zthi, i)
                    pe.wait_ge(s_ztlo, i)
                    after(pe, s_osb, 2 * (i - 1))
                    for k in range(2):
                        cols = slice(k * 512, (k + 1) * 512)
                        for c in range(JC):
                            mm = three(p_out[:, k, :], zt_hi[:, c, :], zt_lo[:, c, :], b_hi[:, c, cols], b_lo[:, c, cols],
                                       c == 0, c == JC - 1)
                        mm.then_inc(s_out, 1)

            pe.wait_ge(s_const, 2)
            pe.wait_ge(s_wc, 2)
            for s in range(2):
                for r in range(R):
                    mm = nc.tensor.transpose(p_out[:, s, r * CO:(r + 1) * CO], w_cut[:, s, r, :], ident[0:CO, 0:CO])
                mm.then_inc(s_wt, 1)
            pe.wait_ge(s_small[0], 32)
            nc.tensor.transpose(p_s[:, CWT], cw_nat[:], ident[:]).then_inc(s_st, 1)
            pe.wait_ge(s_small[2], 16)
            nc.tensor.transpose(p_s[:, CT], c_nat[:], ident[0:N, 0:N]).then_inc(s_st, 1)
            pe.wait_ge(s_small[3], 16)
            nc.tensor.transpose(p_s[0:RD, KT], keys_nat[:], ident[0:E, 0:E]).then_inc(s_st, 1)
            pe.wait_ge(s_sc, 3)
            nc.tensor.matmul(p_s[:, U], cw_t[:], c_t[:], start=True, stop=True).then_inc(s_up, 1)
            pe.wait_ge(s_whi, 2)
            pe.wait_ge(s_wlo, 2)
            conv(0)
            for r in range(R):
                if r >= 3:
                    pe.wait_ge(s_ahi, r - 2)
                    pe.wait_ge(s_alo, r - 2)
                for c in range(JC):
                    if r == 0:
                        pe.wait_ge(s_a[c], 16)
                    mm = nc.tensor.transpose(a_bank(r)[:, c * P:(c + 1) * P],
                                             a_nat[:, c, :].rearrange("j (b r) -> j r b", r=R)[:, r, :], ident[:])
                mm.then_inc(s_at, 1)
            pe.wait_ge(s_small[4], 16)
            for r in range(R):
                mm = nc.tensor.transpose(p_out[:, 0, r * RD:(r + 1) * RD],
                                         wq_nat[:].rearrange("q (b r) -> q r b", r=R)[:, r, :], ident[0:RD, 0:RD])
            mm.then_inc(s_at, 1)
            pe.wait_ge(s_dg, JC + 1)
            for c in range(JC):
                nc.tensor.matmul(p_out[:, 1, c * P:(c + 1) * P], ones[:], diag[:, c * P:(c + 1) * P],
                                 start=True, stop=True)
            pe.wait_ge(s_u, 2)
            nc.tensor.matmul(p_s[:, 0:RD], ones[0:RD, :], diag[0:RD, J:JQ],
                             start=True, stop=True).then_inc(s_bcp, 1)
            pe.wait_ge(s_ahi, R + 1)
            pe.wait_ge(s_alo, R + 1)
            body(0)
            pe.wait_ge(s_bc, 2)
            for n in range(2 * JC):
                if n >= 2:
                    pe.wait_ge(s_bhi, n - 1)
                    pe.wait_ge(s_blo, n - 1)
                for c in range(4):
                    o = 4 * (n % 2) + c
                    if n < 2 and c % 2 == 0:
                        pe.wait_ge(s_b[o // 2], 16)
                    mm = nc.tensor.transpose(p_out[:, n % 2, c * P:(c + 1) * P],
                                             b_nat[:, o // 2, o % 2 * J + n // 2 * P:o % 2 * J + (n // 2 + 1) * P],
                                             ident[:])
                mm.then_inc(s_bt, 1)
            pe.wait_ge(s_bhi, 2 * JC)
            pe.wait_ge(s_blo, 2 * JC)
            body(1)
            with pe.Fori(2, NT - 1) as i:
                body(i)
            body(NT - 1)
            body(NT)

        @block.vector
        def _(dve):
            def low(dst, src, hi, s):
                nc.vector.tensor_tensor(dst, src, hi.bitcast(F32), ALU.subtract).then_inc(s, 1)

            def split_x(t):
                dve.wait_ge(s_xhi, t + 1)
                low(x_lo[:], x_blk[:], x_hi[:], s_xlo)

            def split_h(t):
                for k in range(2):
                    dve.wait_ge(s_hhi, 2 * t + k + 1)
                    at = (slice(None), slice(None), slice(k * P // 2, (k + 1) * P // 2))
                    low(h_lo[at].rearrange("b r (g c) -> b g r c", c=CI),
                        p_conv[:, k, :].rearrange("b (g r c) -> b g r c", r=R, c=CI),
                        h_hi[at].rearrange("b r (g c) -> b g r c", c=CI), s_hlo)

            STEPS = 7

            def gate(i):
                def step(n):
                    dve.wait_ge(s_dve, STEPS * i + n)

                def step_alone(n):
                    step(n)
                    dve.sem_inc(s_alone, 1)

                dve.wait_ge(s_scp, i + 1)
                nc.vector.tensor_copy(sc[:], p_s[:, SC]).then_inc(s_dve, 1)
                step_alone(1)
                nc.vector.max(top_a[:], sc[:]).then_inc(s_dve, 1)
                step(2)
                nc.vector.tensor_scalar(neg_max[:], top_a[:, 0:1], -1.0, None, ALU.mult).then_inc(s_nm, 1)
                nc.vector.match_replace(sc_a[:], top_a[:], sc[:], TAKEN).then_inc(s_dve, 1)
                step_alone(3)
                nc.vector.max(top_b[:], sc_a[:]).then_inc(s_dve, 1)
                step_alone(4)
                nc.vector.match_replace(sc_b[:], top_b[:], sc_a[:], TAKEN).then_inc(s_dve, 1)
                step(5)
                dve.wait_ge(s_e, i + 1)
                nc.vector.scalar_tensor_tensor(out=e_top[:], in0=sc_b[:], scalar=TAKEN, in1=e_all[:],
                                               op0=ALU.is_equal, op1=ALU.mult, accum_out=e_sum[:]).then_inc(s_dve, 1)
                step(6)
                nc.vector.reciprocal(e_inv[:], e_sum[:]).then_inc(s_dve, 1)
                step(7)
                dve.wait_ge(s_zs, 2 * (i + 1))
                nc.vector.scalar_tensor_tensor(
                    out=z_g[:].rearrange("t (e k) -> t e k", k=RANK),
                    in0=z_s[:].rearrange("t (e k) -> t e k", k=RANK), scalar=e_inv[:, 0:1],
                    in1=e_top[:].unsqueeze(2).to_broadcast([P, E, RANK]), op0=ALU.mult, op1=ALU.mult).then_inc(s_zg, 1)

            def add_u(i, dst, cols, src, s):
                nc.vector.scalar_tensor_tensor(out=dst, in0=sum_bc[:, cols], scalar=u[:, bass.ds(i, 1)], in1=src,
                                               op0=ALU.mult, op1=ALU.add).then_inc(s, 1)

            def body(i):
                if real(i - 1):
                    dve.wait_ge(s_zthi, i)
                    low(zt_lo[:], p_t[:].rearrange("j (c t) -> j c t", c=JC), zt_hi[:], s_ztlo)
                if real(i):
                    dve.wait_ge(s_zq, i + 1)
                    add_u(i, q_s[:], slice(J, JQ), p_z[:, 1, J - HB:HB], s_q)
                    after(dve, s_zg, i)
                    add_u(i, z_s[:, HB:J], slice(HB, J), p_z[:, 1, 0:J - HB], s_zs)
                    dve.wait_ge(s_z, i + 1)
                    add_u(i, z_s[:, 0:HB], slice(0, HB), p_z[:, 0, 0:HB], s_zs)
                    gate(i)
                if real(i + 1):
                    split_h(i + 1)
                if real(i + 2):
                    split_x(i + 2)
                if real(i - 1):
                    for k in range(2):
                        dve.wait_ge(s_out, 2 * (i - 1) + k + 1)
                        after(dve, s_stored, 16 * (i - 1))
                        cols = slice(k * 512, (k + 1) * 512)
                        nc.vector.tensor_tensor(
                            o_sb[:, cols], p_out[:, k, :],
                            x_all[:, bass.ds(i - 1, 1), PAD + k * 512:PAD + (k + 1) * 512].rearrange("t a l -> t (a l)"),
                            ALU.add).then_inc(s_osb, 1)

            nc.vector.memset(w_pad[:], 0.0).then_inc(s_wz, 1)
            nc.vector.memset(x_all[:, :, 0:PAD], 0.0).then_inc(s_pads, 1)
            nc.vector.memset(x_all[:, :, PAD + L:LP], 0.0).then_inc(s_pads, 1)
            dve.wait_ge(s_w, 16)
            cut_w(nc.vector, 0)
            for s in range(2):
                dve.wait_ge(s_whi, s + 1)
                low(w_lo[:, s].rearrange("k g (r c) -> k r g c", c=CI),
                    p_out[:, s, :].rearrange("k (r g c) -> k r g c", g=G, c=CI),
                    w_hi[:, s].rearrange("k g (r c) -> k r g c", c=CI), s_wlo)
            dve.wait_ge(s_up, 1)
            dve.wait_ge(s_small[1], 32)
            for k in range(NN):
                rows = slice(k * CO, (k + 1) * CO)
                nc.vector.tensor_scalar(u[rows, :], p_s[rows, U].rearrange("c (i n) -> c n i", n=NN)[:, k, :],
                                        bias2[rows, 0:1], None, ALU.add).then_inc(s_u, 1)
            split_x(0)
            split_h(0)
            dve.wait_ge(s_const, 2)
            for c in range(JC):
                dve.wait_ge(s_a[c], 16)
                nc.vector.tensor_reduce(row_sum[:, c:c + 1], a_nat[:, c, :], mybir.AxisListType.X, ALU.add).then_inc(s_rs, 1)
                dve.wait_ge(s_rs, c + 1)
                nc.vector.tensor_scalar(diag[:, c * P:(c + 1) * P], ident[:], row_sum[:, c:c + 1], None,
                                        ALU.mult).then_inc(s_dg, 1)
            dve.wait_ge(s_small[4], 16)
            nc.vector.tensor_reduce(row_sum[0:RD, JC:JC + 1], wq_nat[:], mybir.AxisListType.X, ALU.add).then_inc(s_rs, 1)
            dve.wait_ge(s_rs, JC + 1)
            nc.vector.tensor_scalar(diag[0:RD, J:JQ], ident[0:RD, 0:RD], row_sum[0:RD, JC:JC + 1], None,
                                    ALU.mult).then_inc(s_dg, 1)
            for r in range(R):
                dve.wait_ge(s_ahi, r + 1)
                low(a_lo[:, r, 0:J], a_bank(r), a_hi[:, r, 0:J], s_alo)
            dve.wait_ge(s_ahi, R + 1)
            low(a_lo[:, :, J:JQ], p_out[:, 0, 0:R * RD].rearrange("b (r q) -> b r q", q=RD), a_hi[:, :, J:JQ], s_alo)
            split_x(1)
            dve.wait_ge(s_bc, 2)
            dve.wait_ge(s_u, 2)
            body(0)
            for n in range(2 * JC):
                dve.wait_ge(s_bhi, n + 1)
                cols = slice(n % 2 * 512, (n % 2 + 1) * 512)
                nc.vector.scalar_tensor_tensor(out=b_lo[:, n // 2, cols], in0=p_out[:, n % 2, :], scalar=SCALING,
                                               in1=b_hi[:, n // 2, cols].bitcast(F32), op0=ALU.mult,
                                               op1=ALU.subtract).then_inc(s_blo, 1)
            body(1)
            with dve.Fori(2, NT - 2) as i:
                body(i)
            for i in range(NT - 2, NT + 1):
                body(i)


_INS = ["x", "cond_128", "fside_S_0", "L0_cond_weight", "L0_cond_c_weight", "L0_ffn_A_w", "L0_ffn_B_w",
        "L0_ffn_Wq_w", "L0_ffn_keys"]


def kernel(**inputs):
    import numpy as np
    import concourse.bacc as bacc
    from concourse.bass_utils import run_bass_kernel_spmd

    nc = bacc.Bacc("TRN2", target_bir_lowering=False, num_devices=1)
    arrays, args = {}, []
    for name in _INS:
        a = np.ascontiguousarray(inputs[name])
        arrays[f"in_{name}"] = a
        args.append(nc.dram_tensor(f"in_{name}", a.shape, mybir.dt.from_np(a.dtype), kind="ExternalInput").ap())
    shape = inputs["x"].shape
    args.append(nc.dram_tensor("out_dram", shape, F32, kind="ExternalOutput").ap())
    adaln_ffn(nc, *args)
    r = run_bass_kernel_spmd(nc, [arrays], core_ids=[0])
    return r.results[0]["out_dram"]
```

```python
from contextlib import ExitStack

import concourse.bass as bass
from concourse import mybir

ALU = mybir.AluOpType
ACT = mybir.ActivationFunctionType
F32 = mybir.dt.float32
F32R = mybir.dt.float32r

P = 128
TAKEN = -float(2**127)
SCALING = 2.0


def adaln_ffn(nc, x, cond, bias, conv_w, cond_w, A_w, B_w, Wq_w, keys, out):
    N, C, L = x.shape
    CO, CI, K = conv_w.shape
    G = C // CI
    PAD = K // 2
    R = 8
    NB = L // R
    NM = NB + 1
    LP = R * NM
    NT = N * C // P
    NN = P // C
    NG = NN * G
    J = A_w.shape[0]
    E, RD = keys.shape
    RANK = J // E
    JC = J // P
    JQ = J + RD
    HB = JQ // 2
    OC = L // P
    D = cond.shape[1]
    assert CI * R == P and NB == P and D == P and K <= R + 1 and C == 64 and NN == 2
    assert 2 * HB == JQ and HB <= 512 and HB % RANK == 0 and NT == 16

    x_v = x.rearrange("(i n) c l -> i (n c) l", n=NN)
    out_v = out.rearrange("(i n) c l -> i (n c) l", n=NN)

    with ExitStack() as ctx:
        def sb(name, shape, dt=F32):
            return ctx.enter_context(nc.sbuf_tensor(name, shape, dt))

        def ps(name, shape):
            return ctx.enter_context(nc.psum_tensor(name, shape, F32))

        def sem(name):
            return ctx.enter_context(nc.semaphore(name))

        ident = sb("ident", [P, P])
        ones = sb("ones", [P, P])
        x_all = sb("x_all", [P, NT, LP])
        x_cut = sb("x_cut", [P, R, NM])
        x_blk = sb("x_blk", [P, NG, NM])
        x_hi = sb("x_hi", [P, NG, NM], F32R)
        x_lo = sb("x_lo", [P, NG, NM], F32R)
        w_pad = sb("w_pad", [CO, CI, 3 * R])
        w_cut = sb("w_cut", [CO, 2, R, P])
        w_hi = sb("w_hi", [P, 2, G, R * CI], F32R)
        w_lo = sb("w_lo", [P, 2, G, R * CI], F32R)
        h_sb = sb("h_sb", [P, G, NN, NB])
        h_hi = sb("h_hi", [P, R, P], F32R)
        h_lo = sb("h_lo", [P, R, P], F32R)
        a_hi = sb("a_hi", [P, R, JQ], F32R)
        a_lo = sb("a_lo", [P, R, JQ], F32R)
        b_hi = sb("b_hi", [P, JC, L], F32R)
        b_lo = sb("b_lo", [P, JC, L], F32R)
        wq_nat = sb("wq_nat", [RD, L])
        keys_nat = sb("keys_nat", [E, RD])
        keys_t = sb("keys_t", [RD, E])
        cw_nat = sb("cw_nat", [P, D])
        cw_t = sb("cw_t", [D, P])
        c_nat = sb("c_nat", [N, D])
        c_t = sb("c_t", [D, N])
        bias2 = sb("bias2", [P, 1])
        u = sb("u", [P, NT])
        row_sum = sb("row_sum", [P, JC + 1])
        diag = sb("diag", [P, JQ])
        sum_bc = sb("sum_bc", [P, JQ])
        z_s = sb("z_s", [P, J])
        z_g = sb("z_g", [P, J])
        zt_hi = sb("zt_hi", [P, JC, P], F32R)
        zt_lo = sb("zt_lo", [P, JC, P], F32R)
        q_s = sb("q_s", [P, RD])
        q_t = sb("q_t", [RD, P])
        sc = sb("sc", [P, E])
        sc_a = sb("sc_a", [P, E])
        sc_b = sb("sc_b", [P, E])
        top_a = sb("top_a", [P, 8])
        top_b = sb("top_b", [P, 8])
        neg_max = sb("neg_max", [P, 1])
        e_all = sb("e_all", [P, E])
        e_top = sb("e_top", [P, E])
        e_sum = sb("e_sum", [P, 1])
        e_inv = sb("e_inv", [P, 1])
        o_sb = sb("o_sb", [P, L])

        A_AT, B_AT = NT - 2 * JC, NT - JC
        a_nat = x_all[:, A_AT:A_AT + JC, PAD:PAD + L]
        b_nat = x_all[:, B_AT:NT, PAD:PAD + L]

        p_conv = ps("p_conv", [P, 2, 512])
        p_z = ps("p_z", [P, 2, 512])
        p_out = ps("p_out", [P, 2, 512])
        p_t = ps("p_t", [P, 512])
        p_h = ps("p_h", [P, 512])
        QT, SC = slice(HB, HB + P), slice(HB + P, HB + P + E)
        CWT, CT, KT, U, WQT = (slice(a, a + n) for a, n in ((0, P), (128, N), (160, E), (224, N), (256, R * RD)))

        def a_bank(r):
            return (p_out[:, 0, :], p_out[:, 1, :], p_t[:])[r % 3]

        def h_bank(t, n):
            return p_z[:, 0, :] if n == 1 and isinstance(t, int) and t < 2 else p_h[:]

        def tokens(h, n):
            return h[:, :, n * C:(n + 1) * C].rearrange("b r (g c) -> b g r c", c=CI)

        s_const = sem("s_const")
        s_iz = sem("s_iz")
        s_pads = sem("s_pads")
        s_wz = sem("s_wz")
        s_w = sem("s_w")
        s_small = [sem(f"s_small{k}") for k in range(6)]
        s_a = [sem(f"s_a{k}") for k in range(JC)]
        s_b = [sem(f"s_b{k}") for k in range(JC)]
        s_x0 = [sem(f"s_x0{k}") for k in range(4)]
        s_x = sem("s_x")
        s_cut = sem("s_cut")
        s_blk0 = [sem(f"s_blk0{g}") for g in range(G)]
        s_blk = sem("s_blk")
        s_xhi = sem("s_xhi")
        s_xlo = sem("s_xlo")
        s_wt = sem("s_wt")
        s_wc = sem("s_wc")
        s_whi = sem("s_whi")
        s_wlo = sem("s_wlo")
        s_st = sem("s_st")
        s_sc = sem("s_sc")
        s_up = sem("s_up")
        s_u = sem("s_u")
        s_at = sem("s_at")
        s_wqt = sem("s_wqt")
        s_wqhi = sem("s_wqhi")
        s_wqlo = sem("s_wqlo")
        s_ahi = sem("s_ahi")
        s_alo = sem("s_alo")
        s_rs = [sem(f"s_rs{c}") for c in range(JC + 1)]
        s_dg = sem("s_dg")
        s_bcp = sem("s_bcp")
        s_bc = sem("s_bc")
        s_bt = sem("s_bt")
        s_bhi = sem("s_bhi")
        s_blo = sem("s_blo")
        s_conv = sem("s_conv")
        s_hc = sem("s_hc")
        s_ht = sem("s_ht")
        s_hhi = sem("s_hhi")
        s_hlo = sem("s_hlo")
        s_zq = sem("s_zq")
        s_z = sem("s_z")
        s_zs = sem("s_zs")
        s_q = sem("s_q")
        s_qtp = sem("s_qtp")
        s_qt = sem("s_qt")
        s_scp = sem("s_scp")
        s_nm = sem("s_nm")
        s_e = sem("s_e")
        s_dve = sem("s_dve")
        s_alone = sem("s_alone")
        s_zg = sem("s_zg")
        s_ztp = sem("s_ztp")
        s_zthi = sem("s_zthi")
        s_ztlo = sem("s_ztlo")
        s_out = sem("s_out")
        s_osb = sem("s_osb")
        s_stored = sem("s_stored")

        block = ctx.enter_context(nc.Block())

        def real(t):
            return not isinstance(t, int) or 0 <= t < NT

        def after(eng, s, count):
            if not isinstance(count, int) or count > 0:
                eng.wait_ge(s, count)

        def real(t):
            return not isinstance(t, int) or 0 <= t < NT

        def after(eng, s, count):
            if not isinstance(count, int) or count > 0:
                eng.wait_ge(s, count)

        def splits(t):
            return t + G

        def w_shift(s, r):
            at = R * s - r + R
            return w_cut[:, s, r, :].rearrange("o (c p) -> o c p", p=R), w_pad[:, :, at:at + R]

        def by_phase(t):
            return x_all[:, t, :].rearrange("c (m p) -> c p m", p=R)

        def relay(eng, n, g, s):
            at = (n * G + g) * CI
            eng.dma_start(x_blk[:, g * NN + n, :], x_cut[at:at + CI]).then_inc(s, 16)

        @block.sync
        def _(sp):
            def load_x(t, s):
                sp.dma_start(x_all[:, t, PAD:PAD + L], x_v[t]).then_inc(s, 16)

            def load_a(c):
                sp.dma_start(a_nat[:, c, :], A_w[c * P:(c + 1) * P, :]).then_inc(s_a[c], 16)

            def relayout(t):
                sp.wait_ge(s_cut, t + 1)
                sp.wait_ge(s_xhi, splits(t - 1))
                sp.wait_ge(s_xlo, splits(t - 1))
                for g in range(G):
                    for n in range(NN):
                        relay(sp, n, g, s_blk)

            def body(i):
                if not isinstance(i, int):
                    sp.lower_val(splits(i + 1))
                    sp.lower_val(i + 3)
                if real(i + 2):
                    relayout(i + 2)
                if real(i + 4):
                    after(sp, s_x, 16 * i)
                    load_x(i + 4, s_x)
                if isinstance(i, int) and i == NT:
                    for k in range(2):
                        cols = slice(k * 512, (k + 1) * 512)
                        sp.wait_ge(s_osb, 2 * (i - 1) + k + 1)
                        sp.dma_start(out_v[i - 1][:, cols], o_sb[:, cols]).then_inc(s_stored, 16)
                elif real(i - 1):
                    sp.wait_ge(s_osb, 2 * i)
                    sp.dma_start(out_v[i - 1], o_sb[:]).then_inc(s_stored, 16)

            load_x(0, s_x0[0])
            sp.wait_ge(s_wz, 1)
            sp.dma_start(w_pad[:, :, R:R + K], conv_w).then_inc(s_w, 16)
            load_a(0)
            load_a(1)
            sp.wait_ge(s_cut, 1)
            for g in range(G):
                for n in range(NN):
                    relay(sp, n, g, s_blk0[g])
                if g < JC - 2:
                    load_a(g + 2)
            load_x(1, s_x0[1])
            for k in range(JC):
                sp.dma_start(b_nat[:, k, :].rearrange("o (c j) -> o c j", c=2),
                             B_w[2 * k * P:2 * (k + 1) * P, :].rearrange("(c o) j -> o c j", c=2)).then_inc(s_b[k], 16)
            relayout(1)
            load_x(2, s_x0[2])
            load_x(3, s_x0[3])
            body(0)
            body(1)
            sp.wait_ge(s_at, R)
            sp.wait_ge(s_bt, 2 * JC)
            sp.wait_ge(s_rs[JC - 1], 1)
            with sp.Fori(2, NT - 4) as i:
                body(i)
            for i in range(NT - 4, NT + 1):
                body(i)
            sp.wait_ge(s_stored, 16 * (NT + 1))

        @block.gpsimd
        def _(pool):
            nc.gpsimd.memset(ident[:], 0.0).then_inc(s_iz, 1)
            nc.gpsimd.memset(ones[:], 1.0).then_inc(s_const, 1)
            pool.wait_ge(s_iz, 1)
            nc.gpsimd.affine_select(out=ident[:], in_=ident[:], compare_op=ALU.not_equal, fill=1.0, base=0,
                                    pattern=[[-1, P]], channel_multiplier=1).then_inc(s_const, 1)
            pool.dma_start(wq_nat[:], Wq_w).then_inc(s_small[4], 16)
            for k in range(NN):
                pool.dma_start(cw_nat[k * CO:(k + 1) * CO, :], cond_w).then_inc(s_small[0], 16)
            pool.dma_start(c_nat[:], cond).then_inc(s_small[2], 16)
            pool.dma_start(keys_nat[:], keys).then_inc(s_small[3], 16)
            for k in range(NN):
                pool.dma_start(bias2[k * CO:(k + 1) * CO, :], bias.rearrange("(o a) -> o a", a=1)).then_inc(s_small[1], 16)
            pool.wait_ge(s_pads, 2)

            def cut(t):
                if isinstance(t, int):
                    pool.wait_ge(s_x0[t], 16)
                else:
                    pool.wait_ge(s_x, 16 * (t - 3))
                pool.wait_ge(s_blk, 16 * NG * (t - 1))
                nc.gpsimd.tensor_copy(x_cut[:], by_phase(t)).then_inc(s_cut, 1)

            cut(2)
            cut(3)
            with pool.Fori(4, NT) as t:
                cut(t)

        @block.scalar
        def _(act):
            def high(dst, src, s, scale=1.0):
                nc.scalar.activation(dst, src, ACT.Copy, scale=scale).then_inc(s, 1)

            def split_x(t):
                act.wait_ge(s_blk, 16 * NG * t)
                act.wait_ge(s_conv, 2 * t)
                high(x_hi[:], x_blk[:], s_xhi)

            def copy_h(t):
                for k in range(2):
                    act.wait_ge(s_conv, 2 * t + k + 1)
                    high(h_sb[:, k * G // 2:(k + 1) * G // 2], p_conv[:, k, :].rearrange("k (g n b) -> k g n b", n=NN, b=NB), s_hc)

            def split_h(t, n):
                act.wait_ge(s_ht, 2 * t + n + 1)
                high(tokens(h_hi, n), h_bank(t, n).rearrange("b (g r c) -> b g r c", r=R, c=CI), s_hhi)

            def split_z(t):
                act.wait_ge(s_ztp, t + 1)
                after(act, s_out, 2 * t)
                high(zt_hi[:], p_t[:].rearrange("j (c t) -> j c t", c=JC), s_zthi)

            def copy_q(i):
                act.wait_ge(s_qtp, i + 1)
                nc.scalar.activation(q_t[:], p_z[0:RD, 1, QT], ACT.Copy).then_inc(s_qt, 1)

            def exp(i):
                act.wait_ge(s_nm, i + 1)
                nc.scalar.activation(e_all[:], sc[:], ACT.Exp, bias=neg_max[:]).then_inc(s_e, 1)

            def body(i):
                if isinstance(i, int) and i == 1:
                    b_high(5)
                elif real(i - 1):
                    split_z(i - 1)
                if real(i):
                    copy_q(i)
                    if isinstance(i, int) and i == 1:
                        split_z(0)
                        b_high(6)
                        b_high(7)
                    exp(i)
                if real(i + 1):
                    copy_h(i + 1)
                    split_h(i + 1, 0)
                    split_h(i + 1, 1)
                if real(i + 2):
                    split_x(i + 2)

            def b_high(n):
                act.wait_ge(s_bt, n + 1)
                high(b_hi[:, n // 2, n % 2 * 512:(n % 2 + 1) * 512], p_out[:, n % 2, :], s_bhi, SCALING)

            act.wait_ge(s_w, 16)
            for r in range(R):
                dst, src = w_shift(1, r)
                high(dst, src, s_wc)
            for s in range(2):
                act.wait_ge(s_wt, s + 1)
                high(w_hi[:, s].rearrange("k g (r c) -> k r g c", c=CI),
                     p_out[:, s, :].rearrange("k (r g c) -> k r g c", g=G, c=CI), s_whi)
            def row_sums(c):
                act.wait_ge(s_a[c], 16)
                nc.scalar.activation(b_hi[:, c, :], a_nat[:, c, :], ACT.Copy, accum_out=row_sum[:, c:c + 1]).then_inc(s_rs[c], 1)

            for g in range(G):
                act.wait_ge(s_blk0[g], 16 * NN)
                high(x_hi[:, g * NN:(g + 1) * NN], x_blk[:, g * NN:(g + 1) * NN], s_xhi)
                if g == 1:
                    row_sums(1)
            act.wait_ge(s_st, 4)
            nc.scalar.activation(cw_t[:], p_t[:, CWT], ACT.Copy).then_inc(s_sc, 1)
            nc.scalar.activation(c_t[:], p_t[:, CT], ACT.Copy).then_inc(s_sc, 1)
            nc.scalar.activation(keys_t[:], p_t[0:RD, KT], ACT.Copy).then_inc(s_sc, 1)
            high(a_hi[:, :, J:JQ], p_t[:, WQT].rearrange("b (r q) -> b r q", q=RD), s_wqhi)
            copy_h(0)
            for r in range(R):
                if r < NN:
                    split_h(0, r)
                act.wait_ge(s_at, r + 1)
                high(a_hi[:, r, 0:J], a_bank(r), s_ahi)
                if r == 2 or r == 3:
                    row_sums(r)
            split_x(1)
            b_high(0)
            b_high(1)
            act.wait_ge(s_bcp, 1)
            nc.scalar.activation(sum_bc[:, 0:J], p_conv[:, 0, :], ACT.Copy).then_inc(s_bc, 1)
            nc.scalar.activation(sum_bc[:, J:JQ], p_conv[:, 1, 0:RD], ACT.Copy).then_inc(s_bc, 1)
            b_high(2)
            copy_q(0)
            copy_h(1)
            b_high(3)
            split_h(1, 0)
            b_high(4)
            split_h(1, 1)
            exp(0)
            split_x(2)
            body(1)
            with act.Fori(2, NT - 2) as i:
                body(i)
            for i in range(NT - 2, NT + 1):
                body(i)

        @block.tensor
        def _(pe):
            def three(dst, s_hi, s_lo, m_hi, m_lo, first, last):
                nc.tensor.matmul(dst, s_hi, m_hi, start=first, stop=False)
                nc.tensor.matmul(dst, s_hi, m_lo, start=False, stop=False)
                return nc.tensor.matmul(dst, s_lo, m_hi, start=False, stop=last)

            def conv_group(g):
                k, at = g * 2 // G, g % (G // 2) * NN * NB
                for s in range(2):
                    blocks = (slice(None), slice(g * NN, (g + 1) * NN), slice(s, s + NB))
                    mm = three(p_conv[:, k, at:at + NN * NB], w_hi[:, s, g, :], w_lo[:, s, g, :],
                               x_hi[blocks], x_lo[blocks], s == 0, s == 1)
                if g % (G // 2) == G // 2 - 1:
                    mm.then_inc(s_conv, 1)

            def conv(t):
                pe.wait_ge(s_xhi, splits(t))
                pe.wait_ge(s_xlo, splits(t))
                for g in range(G):
                    conv_group(g)

            def turn_h(t, n):
                if n == 0:
                    pe.wait_ge(s_hc, 2 * (t + 1))
                elif isinstance(t, int) and t < 2:
                    after(pe, s_zs, 2 * t)
                else:
                    pe.wait_ge(s_hhi, 2 * t + 1)
                    pe.wait_ge(s_hlo, 2 * t + 1)
                for g in range(G):
                    mm = nc.tensor.transpose(h_bank(t, n)[:, g * P:(g + 1) * P], h_sb[:, g, n, :], ident[:])
                mm.then_inc(s_ht, 1)

            def z_bank(k, phases):
                for r in phases:
                    cols = slice(k * HB, (k + 1) * HB)
                    mm = three(p_z[:, k, 0:HB], h_hi[:, r, :], h_lo[:, r, :], a_hi[:, r, cols], a_lo[:, r, cols],
                               r == 0, r == R - 1)
                return mm

            def turn_q(i):
                pe.wait_ge(s_q, i + 1)
                pe.wait_ge(s_zs, 2 * i + 1)
                nc.tensor.transpose(p_z[0:RD, 1, QT], q_s[:], ident[:]).then_inc(s_qtp, 1)

            def scores(i):
                pe.wait_ge(s_qt, i + 1)
                nc.tensor.matmul(p_z[:, 1, SC], q_t[:], keys_t[:], start=True, stop=True).then_inc(s_scp, 1)

            def turn_z(t):
                pe.wait_ge(s_zg, t + 1)
                for c in range(JC):
                    mm = nc.tensor.transpose(p_t[:, c * P:(c + 1) * P], z_g[:, c * P:(c + 1) * P], ident[:])
                mm.then_inc(s_ztp, 1)

            def out_part(k, chunks):
                cols = slice(k * 512, (k + 1) * 512)
                for c in chunks:
                    mm = three(p_out[:, k, :], zt_hi[:, c, :], zt_lo[:, c, :], b_hi[:, c, cols], b_lo[:, c, cols],
                               c == 0, c == JC - 1)
                if c == JC - 1:
                    mm.then_inc(s_out, 1)

            def body(i):
                if isinstance(i, int) and i == 1:
                    turn_b(5)
                    pe.wait_ge(s_dve, 1)
                elif real(i - 1):
                    turn_z(i - 1)
                if real(i):
                    pe.wait_ge(s_hhi, 2 * (i + 1))
                    pe.wait_ge(s_hlo, 2 * (i + 1))
                    z_bank(1, range(R)).then_inc(s_zq, 1)
                    z_bank(0, range(R // 2))
                    turn_q(i)
                    z_bank(0, range(R // 2, R)).then_inc(s_z, 1)
                    scores(i)
                    if isinstance(i, int) and i == 1:
                        turn_z(0)
                        turn_b(6)
                        turn_b(7)
                if real(i + 1):
                    conv(i + 1)
                if isinstance(i, int) and i == 1:
                    pe.wait_ge(s_bhi, 2 * JC)
                    pe.wait_ge(s_blo, 2 * JC)
                if real(i - 1):
                    pe.wait_ge(s_zthi, i)
                    pe.wait_ge(s_ztlo, i)
                    after(pe, s_osb, 2 * (i - 1))
                    out_part(0, range(JC // 2))
                if real(i + 1):
                    turn_h(i + 1, 0)
                if real(i - 1):
                    out_part(0, range(JC // 2, JC))
                    out_part(1, range(1))
                if real(i + 1):
                    turn_h(i + 1, 1)
                if real(i - 1):
                    out_part(1, range(1, JC))

            def turn_a(r):
                if r >= 3:
                    pe.wait_ge(s_ahi, r - 2)
                    pe.wait_ge(s_alo, r - 2)
                for c in range(JC):
                    if r == 0:
                        pe.wait_ge(s_a[c], 16)
                    mm = nc.tensor.transpose(a_bank(r)[:, c * P:(c + 1) * P],
                                             a_nat[:, c, :].rearrange("j (b r) -> j r b", r=R)[:, r, :], ident[:])
                mm.then_inc(s_at, 1)

            def turn_b(n):
                if n < 2:
                    pe.wait_ge(s_ahi, R - 1 + n)
                    pe.wait_ge(s_alo, R - 1 + n)
                else:
                    pe.wait_ge(s_bhi, n - 1)
                    pe.wait_ge(s_blo, n - 1)
                for c in range(4):
                    o = 4 * (n % 2) + c
                    if n < 2 and c % 2 == 0:
                        pe.wait_ge(s_b[o // 2], 16)
                    mm = nc.tensor.transpose(p_out[:, n % 2, c * P:(c + 1) * P],
                                             b_nat[:, o // 2, o % 2 * J + n // 2 * P:o % 2 * J + (n // 2 + 1) * P],
                                             ident[:])
                mm.then_inc(s_bt, 1)

            pe.wait_ge(s_const, 2)
            pe.wait_ge(s_wc, 2 * R)
            for s in range(2):
                for r in range(R):
                    mm = nc.tensor.transpose(p_out[:, s, r * CO:(r + 1) * CO], w_cut[:, s, r, :], ident[0:CO, 0:CO])
                mm.then_inc(s_wt, 1)
            pe.wait_ge(s_small[4], 16)
            for r in range(R):
                mm = nc.tensor.transpose(p_t[:, WQT.start + r * RD:WQT.start + (r + 1) * RD],
                                         wq_nat[:].rearrange("q (b r) -> q r b", r=R)[:, r, :], ident[0:RD, 0:RD])
            mm.then_inc(s_st, 1)
            pe.wait_ge(s_small[0], 32)
            nc.tensor.transpose(p_t[:, CWT], cw_nat[:], ident[:]).then_inc(s_st, 1)
            pe.wait_ge(s_small[2], 16)
            nc.tensor.transpose(p_t[:, CT], c_nat[:], ident[0:N, 0:N]).then_inc(s_st, 1)
            pe.wait_ge(s_small[3], 16)
            nc.tensor.transpose(p_t[0:RD, KT], keys_nat[:], ident[0:E, 0:E]).then_inc(s_st, 1)
            pe.wait_ge(s_whi, 2)
            pe.wait_ge(s_wlo, 2)
            for g in range(G):
                pe.wait_ge(s_xhi, g + 1)
                pe.wait_ge(s_xlo, g + 1)
                conv_group(g)
            pe.wait_ge(s_sc, 3)
            pe.wait_ge(s_wqlo, 1)
            nc.tensor.matmul(p_t[:, U], cw_t[:], c_t[:], start=True, stop=True).then_inc(s_up, 1)
            turn_a(0)
            turn_h(0, 0)
            turn_a(1)
            turn_h(0, 1)
            pe.wait_ge(s_u, NN)
            turn_a(2)
            pe.wait_ge(s_hhi, 2)
            pe.wait_ge(s_hlo, 2)
            for r in range(R):
                pe.wait_ge(s_ahi, r + 1)
                pe.wait_ge(s_alo, r + 1)
                z1 = z_bank(1, [r])
                z0 = z_bank(0, [r])
                if r + 3 < R:
                    turn_a(r + 3)
                else:
                    turn_b(r + 3 - R)
                if r == R - 2:
                    for c in range(JC + 1):
                        pe.wait_ge(s_dg, c + 1)
                        rows = P if c < JC else RD
                        dst = p_conv[:, 0, c * P:(c + 1) * P] if c < JC else p_conv[:, 1, 0:RD]
                        mm = nc.tensor.matmul(dst, ones[0:rows, :], diag[0:rows, c * P:c * P + rows], start=True, stop=True)
                    mm.then_inc(s_bcp, 1)
            z1.then_inc(s_zq, 1)
            z0.then_inc(s_z, 1)
            pe.wait_ge(s_xhi, splits(1))
            pe.wait_ge(s_xlo, splits(1))
            pe.wait_ge(s_bc, 2)
            conv_group(0)
            conv_group(1)
            turn_q(0)
            conv_group(2)
            scores(0)
            conv_group(3)
            turn_b(3)
            turn_h(1, 0)
            turn_h(1, 1)
            turn_b(4)
            body(1)
            with pe.Fori(2, NT - 1) as i:
                body(i)
            body(NT - 1)
            body(NT)

        @block.vector
        def _(dve):
            def low(dst, src, hi, s):
                nc.vector.tensor_tensor(dst, src, hi.bitcast(F32), ALU.subtract).then_inc(s, 1)

            def cut(t):
                dve.wait_ge(s_x0[t], 16)
                nc.vector.tensor_copy(x_cut[:], by_phase(t)).then_inc(s_cut, 1)

            def split_x(t):
                dve.wait_ge(s_xhi, splits(t))
                low(x_lo[:], x_blk[:], x_hi[:], s_xlo)

            def split_h(t, n):
                dve.wait_ge(s_hhi, 2 * t + n + 1)
                low(tokens(h_lo, n), h_bank(t, n).rearrange("b (g r c) -> b g r c", r=R, c=CI), tokens(h_hi, n), s_hlo)

            def split_z(t):
                dve.wait_ge(s_zthi, t + 1)
                low(zt_lo[:], p_t[:].rearrange("j (c t) -> j c t", c=JC), zt_hi[:], s_ztlo)

            STEPS = 7

            def copy_scores(i):
                dve.wait_ge(s_scp, i + 1)
                nc.vector.tensor_copy(sc[:], p_z[:, 1, SC]).then_inc(s_dve, 1)

            def gate(i):
                def step(n):
                    dve.wait_ge(s_dve, STEPS * i + n)

                def step_alone(n):
                    step(n)
                    dve.sem_inc(s_alone, 1)

                step_alone(1)
                nc.vector.max(top_a[:], sc[:]).then_inc(s_dve, 1)
                step(2)
                nc.vector.tensor_scalar(neg_max[:], top_a[:, 0:1], -1.0, None, ALU.mult).then_inc(s_nm, 1)
                nc.vector.match_replace(sc_a[:], top_a[:], sc[:], TAKEN).then_inc(s_dve, 1)
                step_alone(3)
                nc.vector.max(top_b[:], sc_a[:]).then_inc(s_dve, 1)
                step_alone(4)
                nc.vector.match_replace(sc_b[:], top_b[:], sc_a[:], TAKEN).then_inc(s_dve, 1)
                step(5)
                dve.wait_ge(s_e, i + 1)
                nc.vector.scalar_tensor_tensor(out=e_top[:], in0=sc_b[:], scalar=TAKEN, in1=e_all[:],
                                               op0=ALU.is_equal, op1=ALU.mult, accum_out=e_sum[:]).then_inc(s_dve, 1)
                step(6)
                nc.vector.reciprocal(e_inv[:], e_sum[:]).then_inc(s_dve, 1)
                step(7)
                dve.wait_ge(s_zs, 2 * (i + 1))
                nc.vector.scalar_tensor_tensor(
                    out=z_g[:].rearrange("t (e k) -> t e k", k=RANK),
                    in0=z_s[:].rearrange("t (e k) -> t e k", k=RANK), scalar=e_inv[:, 0:1],
                    in1=e_top[:].unsqueeze(2).to_broadcast([P, E, RANK]), op0=ALU.mult, op1=ALU.mult).then_inc(s_zg, 1)

            def add_u(i, dst, cols, src, s):
                nc.vector.scalar_tensor_tensor(out=dst, in0=sum_bc[:, cols], scalar=u[:, bass.ds(i, 1)], in1=src,
                                               op0=ALU.mult, op1=ALU.add).then_inc(s, 1)

            def z_out(i):
                dve.wait_ge(s_zq, i + 1)
                add_u(i, q_s[:], slice(J, JQ), p_z[:, 1, J - HB:HB], s_q)
                after(dve, s_zg, i)
                add_u(i, z_s[:, HB:J], slice(HB, J), p_z[:, 1, 0:J - HB], s_zs)
                dve.wait_ge(s_z, i + 1)
                add_u(i, z_s[:, 0:HB], slice(0, HB), p_z[:, 0, 0:HB], s_zs)

            def body(i):
                if isinstance(i, int) and i == 1:
                    b_low(5)
                elif real(i - 1):
                    split_z(i - 1)
                if real(i):
                    z_out(i)
                    copy_scores(i)
                    if isinstance(i, int) and i == 1:
                        split_x(2)
                        split_z(0)
                        b_low(6)
                        b_low(7)
                    gate(i)
                if real(i + 1):
                    split_h(i + 1, 0)
                    split_h(i + 1, 1)
                if real(i - 1):
                    for k in range(2):
                        if k == 1 and real(i + 2):
                            split_x(i + 2)
                        dve.wait_ge(s_out, 2 * (i - 1) + k + 1)
                        after(dve, s_stored, 16 * (i - 1))
                        cols = slice(k * 512, (k + 1) * 512)
                        nc.vector.tensor_tensor(
                            o_sb[:, cols], p_out[:, k, :],
                            x_all[:, bass.ds(i - 1, 1), PAD + k * 512:PAD + (k + 1) * 512].rearrange("t a l -> t (a l)"),
                            ALU.add).then_inc(s_osb, 1)

            def b_low(n):
                dve.wait_ge(s_bhi, n + 1)
                cols = slice(n % 2 * 512, (n % 2 + 1) * 512)
                nc.vector.scalar_tensor_tensor(out=b_lo[:, n // 2, cols], in0=p_out[:, n % 2, :], scalar=SCALING,
                                               in1=b_hi[:, n // 2, cols].bitcast(F32), op0=ALU.mult,
                                               op1=ALU.subtract).then_inc(s_blo, 1)

            def row_sums(rows, src, landed, c):
                dve.wait_ge(landed, 16)
                nc.vector.tensor_reduce(row_sum[0:rows, c:c + 1], src, mybir.AxisListType.X, ALU.add).then_inc(s_rs[c], 1)

            def a_low(r):
                dve.wait_ge(s_ahi, r + 1)
                low(a_lo[:, r, 0:J], a_bank(r), a_hi[:, r, 0:J], s_alo)

            nc.vector.memset(w_pad[:], 0.0).then_inc(s_wz, 1)
            nc.vector.memset(x_all[:, :, 0:PAD], 0.0).then_inc(s_pads, 1)
            nc.vector.memset(x_all[:, :, PAD + L:LP], 0.0).then_inc(s_pads, 1)
            dve.wait_ge(s_pads, 2)
            cut(0)
            dve.wait_ge(s_w, 16)
            for r in range(R):
                dst, src = w_shift(0, r)
                nc.vector.tensor_copy(dst, src).then_inc(s_wc, 1)
            dve.wait_ge(s_const, 2)
            row_sums(RD, wq_nat[:], s_small[4], JC)
            row_sums(P, a_nat[:, 0, :], s_a[0], 0)
            for s in range(2):
                dve.wait_ge(s_whi, s + 1)
                low(w_lo[:, s].rearrange("k g (r c) -> k r g c", c=CI),
                    p_out[:, s, :].rearrange("k (r g c) -> k r g c", g=G, c=CI),
                    w_hi[:, s].rearrange("k g (r c) -> k r g c", c=CI), s_wlo)
            for g in range(G):
                dve.wait_ge(s_xhi, g + 1)
                at = slice(g * NN, (g + 1) * NN)
                low(x_lo[:, at], x_blk[:, at], x_hi[:, at], s_xlo)
            dve.wait_ge(s_wqhi, 1)
            low(a_lo[:, :, J:JQ], p_t[:, WQT].rearrange("b (r q) -> b r q", q=RD), a_hi[:, :, J:JQ], s_wqlo)
            dve.wait_ge(s_up, 1)
            dve.wait_ge(s_small[1], 32)
            for k in range(NN):
                rows = slice(k * CO, (k + 1) * CO)
                nc.vector.tensor_scalar(u[rows, :], p_t[rows, U].rearrange("c (i n) -> c n i", n=NN)[:, k, :],
                                        bias2[rows, 0:1], None, ALU.add).then_inc(s_u, 1)
            cut(1)

            def diagonal(c):
                rows = P if c < JC else RD
                dve.wait_ge(s_rs[c], 1)
                nc.vector.tensor_scalar(diag[0:rows, c * P:c * P + rows], ident[0:rows, 0:rows],
                                        row_sum[0:rows, c:c + 1], None, ALU.mult).then_inc(s_dg, 1)

            for r in range(R):
                if r < NN:
                    split_h(0, r)
                a_low(r)
                if 2 <= r <= JC + 2:
                    diagonal(r - 2)
            split_x(1)
            b_low(0)
            b_low(1)
            dve.wait_ge(s_bc, 2)
            dve.wait_ge(s_u, 2)
            z_out(0)
            b_low(2)
            copy_scores(0)
            split_h(1, 0)
            b_low(3)
            split_h(1, 1)
            gate(0)
            b_low(4)
            body(1)
            with dve.Fori(2, NT - 2) as i:
                body(i)
            for i in range(NT - 2, NT + 1):
                body(i)


_INS = ["x", "cond_128", "fside_S_0", "L0_cond_weight", "L0_cond_c_weight", "L0_ffn_A_w", "L0_ffn_B_w",
        "L0_ffn_Wq_w", "L0_ffn_keys"]


def kernel(**inputs):
    import numpy as np
    import concourse.bacc as bacc
    from concourse.bass_utils import run_bass_kernel_spmd

    nc = bacc.Bacc("TRN2", target_bir_lowering=False, num_devices=1)
    arrays, args = {}, []
    for name in _INS:
        a = np.ascontiguousarray(inputs[name])
        arrays[f"in_{name}"] = a
        args.append(nc.dram_tensor(f"in_{name}", a.shape, mybir.dt.from_np(a.dtype), kind="ExternalInput").ap())
    shape = inputs["x"].shape
    args.append(nc.dram_tensor("out_dram", shape, F32, kind="ExternalOutput").ap())
    adaln_ffn(nc, *args)
    r = run_bass_kernel_spmd(nc, [arrays], core_ids=[0])
    return r.results[0]["out_dram"]
```

```python
from contextlib import ExitStack

import concourse.bass as bass
from concourse import mybir

ALU = mybir.AluOpType
ACT = mybir.ActivationFunctionType
F32 = mybir.dt.float32
F32R = mybir.dt.float32r

P = 128
TAKEN = -float(2**127)
SCALING = 2.0


def adaln_ffn(nc, x, cond, bias, conv_w, cond_w, A_w, B_w, Wq_w, keys, out):
    N, C, L = x.shape
    CO, CI, K = conv_w.shape
    G = C // CI
    PAD = K // 2
    R = 8
    NB = L // R
    NM = NB + 1
    LP = R * NM
    NT = N * C // P
    NN = P // C
    NG = NN * G
    J = A_w.shape[0]
    E, RD = keys.shape
    RANK = J // E
    JC = J // P
    JQ = J + RD
    HB = JQ // 2
    OC = L // P
    D = cond.shape[1]
    assert CI * R == P and NB == P and D == P and K <= R + 1 and C == 64 and NN == 2
    assert 2 * HB == JQ and HB <= 512 and HB % RANK == 0 and NT == 16

    x_v = x.rearrange("(i n) c l -> i (n c) l", n=NN)
    out_v = out.rearrange("(i n) c l -> i (n c) l", n=NN)

    with ExitStack() as ctx:
        def sb(name, shape, dt=F32):
            return ctx.enter_context(nc.sbuf_tensor(name, shape, dt))

        def ps(name, shape):
            return ctx.enter_context(nc.psum_tensor(name, shape, F32))

        def sem(name):
            return ctx.enter_context(nc.semaphore(name))

        ident = sb("ident", [P, P])
        ones = sb("ones", [P, P])
        x_all = sb("x_all", [P, NT, LP])
        x_cut = sb("x_cut", [P, R, NM])
        x_blk = sb("x_blk", [P, NG, NM])
        x_hi = sb("x_hi", [P, NG, NM], F32R)
        x_lo = sb("x_lo", [P, NG, NM], F32R)
        w_pad = sb("w_pad", [CO, CI, 3 * R])
        w_cut = sb("w_cut", [CO, 2, R, P])
        w_hi = sb("w_hi", [P, 2, G, R * CI], F32R)
        w_lo = sb("w_lo", [P, 2, G, R * CI], F32R)
        h_sb = sb("h_sb", [P, G, NN, NB])
        h_hi = sb("h_hi", [P, R, P], F32R)
        h_lo = sb("h_lo", [P, R, P], F32R)
        a_hi = sb("a_hi", [P, R, JQ], F32R)
        a_lo = sb("a_lo", [P, R, JQ], F32R)
        b_hi = sb("b_hi", [P, JC, L], F32R)
        b_lo = sb("b_lo", [P, JC, L], F32R)
        wq_nat = sb("wq_nat", [RD, L])
        keys_nat = sb("keys_nat", [E, RD])
        keys_t = sb("keys_t", [RD, E])
        cw_nat = sb("cw_nat", [P, D])
        cw_t = sb("cw_t", [D, P])
        c_nat = sb("c_nat", [N, D])
        c_t = sb("c_t", [D, N])
        bias2 = sb("bias2", [P, 1])
        u = sb("u", [P, NT])
        row_sum = sb("row_sum", [P, JC + 1])
        diag = sb("diag", [P, JQ])
        sum_bc = sb("sum_bc", [P, JQ])
        z_s = sb("z_s", [P, J])
        z_g = sb("z_g", [P, J])
        zt_hi = sb("zt_hi", [P, JC, P], F32R)
        zt_lo = sb("zt_lo", [P, JC, P], F32R)
        q_s = sb("q_s", [P, RD])
        q_t = sb("q_t", [RD, P])
        sc = sb("sc", [P, E])
        sc_a = sb("sc_a", [P, E])
        sc_b = sb("sc_b", [P, E])
        top_a = sb("top_a", [P, 8])
        top_b = sb("top_b", [P, 8])
        neg_max = sb("neg_max", [P, 1])
        e_all = sb("e_all", [P, E])
        e_top = sb("e_top", [P, E])
        e_sum = sb("e_sum", [P, 1])
        e_inv = sb("e_inv", [P, 1])

        A_AT, B_AT = NT - 2 * JC, NT - JC
        a_nat = x_all[:, A_AT:A_AT + JC, PAD:PAD + L]
        b_nat = x_all[:, B_AT:NT, PAD:PAD + L]

        p_conv = ps("p_conv", [P, 2, 512])
        p_z = ps("p_z", [P, 2, 512])
        p_out = ps("p_out", [P, 2, 512])
        p_t = ps("p_t", [P, 512])
        p_h = ps("p_h", [P, 512])
        QT, SC = slice(HB, HB + P), slice(HB + P, HB + P + E)
        CWT, CT, KT, U, WQT = (slice(a, a + n) for a, n in ((0, P), (128, N), (160, E), (224, N), (256, R * RD)))

        def a_bank(r):
            return (p_out[:, 0, :], p_out[:, 1, :], p_t[:])[r % 3]

        def zt(t):
            return (h_hi[:, 0:JC], h_lo[:, 0:JC]) if isinstance(t, int) and t == NT - 1 else (zt_hi[:], zt_lo[:])

        def tile_cols(t, lo, hi):
            return x_all[:, bass.ds(t, 1), PAD + lo:PAD + hi].rearrange("t a l -> t (a l)")

        def parts(t):
            if isinstance(t, int) and t == NT - 1:
                return ((p_out[:, 0, :], 0, 512), (p_out[:, 1, 0:256], 512, 768), (p_z[:, 0, 0:256], 768, 1024))
            return ((p_out[:, 0, :], 0, 512), (p_out[:, 1, :], 512, 1024))

        def h_views(t, k, *hs):
            def places(n, groups):
                return [h[:, :, n * C:(n + 1) * C].rearrange("b r (g c) -> b g r c", c=CI)[:, groups] for h in hs]

            if not early(t):
                return [(p_h[:].rearrange("b (g r c) -> b g r c", r=R, c=CI), *places(k, slice(0, G)))]
            bank = (p_h[:], p_z[:, 0, :])[k].rearrange("b (n g r c) -> b n g r c", n=NN, r=R, c=CI)
            return [(bank[:, n], *places(n, slice(2 * k, 2 * (k + 1)))) for n in range(NN)]

        def early(t):
            return isinstance(t, int) and t < 2

        BY_SP = 5
        WARM = (12, 6)

        s_const = sem("s_const")
        s_iz = sem("s_iz")
        s_pads = sem("s_pads")
        s_wz = sem("s_wz")
        s_w = sem("s_w")
        s_small = [sem(f"s_small{k}") for k in range(5)]
        s_a = [sem(f"s_a{k}") for k in range(JC)]
        s_b = [sem(f"s_b{k}") for k in range(JC)]
        s_x0 = [sem(f"s_x0{k}") for k in range(4)]
        s_x = sem("s_x")
        s_cut = sem("s_cut")
        s_blk0 = [sem(f"s_blk0{k}") for k in range(NG)]
        s_blk = sem("s_blk")
        s_xhi = sem("s_xhi")
        s_xlo = sem("s_xlo")
        s_wt = sem("s_wt")
        s_wc = [sem(f"s_wc{s}") for s in range(2)]
        s_whi = sem("s_whi")
        s_wlo = sem("s_wlo")
        s_st = sem("s_st")
        s_sc = sem("s_sc")
        s_up = sem("s_up")
        s_u = sem("s_u")
        s_at = sem("s_at")
        s_wqhi = sem("s_wqhi")
        s_wqlo = sem("s_wqlo")
        s_ahi = sem("s_ahi")
        s_alo = sem("s_alo")
        s_rs = [sem(f"s_rs{c}") for c in range(JC + 1)]
        s_dg = sem("s_dg")
        s_bcp = sem("s_bcp")
        s_bc = sem("s_bc")
        s_bt = sem("s_bt")
        s_bhi = sem("s_bhi")
        s_blo = sem("s_blo")
        s_conv = sem("s_conv")
        s_hc = sem("s_hc")
        s_ht = sem("s_ht")
        s_hhi = sem("s_hhi")
        s_hlo = sem("s_hlo")
        s_zq = sem("s_zq")
        s_z = sem("s_z")
        s_zs = sem("s_zs")
        s_q = sem("s_q")
        s_qtp = sem("s_qtp")
        s_qt = sem("s_qt")
        s_scp = sem("s_scp")
        s_nm = sem("s_nm")
        s_e = sem("s_e")
        s_dve = sem("s_dve")
        s_alone = sem("s_alone")
        s_zg = sem("s_zg")
        s_ztp = sem("s_ztp")
        s_zthi = sem("s_zthi")
        s_ztlo = sem("s_ztlo")
        s_out = sem("s_out")
        s_added = sem("s_added")
        s_stored = sem("s_stored")

        block = ctx.enter_context(nc.Block())

        def real(t):
            return not isinstance(t, int) or 0 <= t < NT

        def after(eng, s, count):
            if not isinstance(count, int) or count > 0:
                eng.wait_ge(s, count)

        def splits(t):
            return t + G

        W_DVE = (R // 2, R // 2 + 1)

        def w_shift(s, r):
            at = R * s - r + R
            return w_cut[:, s, r, :].rearrange("o (c p) -> o c p", p=R), w_pad[:, :, at:at + R]

        def by_phase(t):
            return x_all[:, t, :].rearrange("c (m p) -> c p m", p=R)

        def relay(eng, n, g, s):
            at = (n * G + g) * CI
            eng.dma_start(x_blk[:, g * NN + n, :], x_cut[at:at + CI]).then_inc(s, 16)

        def load_a(eng, c):
            eng.dma_start(a_nat[:, c, :], A_w[c * P:(c + 1) * P, :]).then_inc(s_a[c], 16)

        @block.sync
        def _(sp):
            def load_x(t, s):
                sp.dma_start(x_all[:, t, PAD:PAD + L], x_v[t]).then_inc(s, 16)

            def relayout(t):
                sp.wait_ge(s_cut, t + 1)
                sp.wait_ge(s_xhi, splits(t - 1))
                sp.wait_ge(s_xlo, splits(t - 1))
                for g in range(G):
                    for n in range(NN):
                        relay(sp, n, g, s_blk)

            def body(i):
                if not isinstance(i, int):
                    sp.lower_val(splits(i + 1))
                    sp.lower_val(i + 3)
                if real(i + 2):
                    relayout(i + 2)
                if real(i + 4):
                    after(sp, s_x, 16 * i)
                    load_x(i + 4, s_x)
                if isinstance(i, int) and i == NT:
                    for k, (_, lo, hi) in enumerate(parts(i - 1)):
                        sp.wait_ge(s_added, 2 * (i - 1) + k + 1)
                        sp.dma_start(out_v[i - 1][:, lo:hi], tile_cols(i - 1, lo, hi)).then_inc(s_stored, 16)
                elif real(i - 1):
                    sp.wait_ge(s_added, 2 * i)
                    sp.dma_start(out_v[i - 1], tile_cols(i - 1, 0, L)).then_inc(s_stored, 16)

            load_x(0, s_x0[0])
            sp.wait_ge(s_wz, 1)
            sp.dma_start(w_pad[:, :, R:R + K], conv_w).then_inc(s_w, 16)
            load_a(sp, 0)
            load_a(sp, 1)
            sp.dma_start(c_nat[:], cond).then_inc(s_small[2], 16)
            sp.dma_start(keys_nat[:], keys).then_inc(s_small[3], 16)
            sp.wait_ge(s_cut, 1)
            for k in range(BY_SP):
                relay(sp, k % NN, k // NN, s_blk0[k])
            load_a(sp, 2)
            load_a(sp, 3)
            load_x(1, s_x0[1])
            for k in range(JC):
                sp.dma_start(b_nat[:, k, :].rearrange("o (c j) -> o c j", c=2),
                             B_w[2 * k * P:2 * (k + 1) * P, :].rearrange("(c o) j -> o c j", c=2)).then_inc(s_b[k], 16)
            relayout(1)
            load_x(2, s_x0[2])
            load_x(3, s_x0[3])
            body(0)
            body(1)
            sp.wait_ge(s_at, R)
            sp.wait_ge(s_bt, 2 * JC)
            sp.wait_ge(s_rs[JC - 1], 1)
            with sp.Fori(2, NT - 4) as i:
                body(i)
            for i in range(NT - 4, NT + 1):
                body(i)
            sp.wait_ge(s_stored, 16 * (NT - 1 + len(parts(NT - 1))))

        @block.gpsimd
        def _(pool):
            nc.gpsimd.memset(ones[:], 1.0).then_inc(s_const, 1)
            nc.gpsimd.memset(ident[:], 0.0).then_inc(s_iz, 1)
            pool.wait_ge(s_iz, 1)
            nc.gpsimd.affine_select(out=ident[:], in_=ident[:], compare_op=ALU.not_equal, fill=1.0, base=0,
                                    pattern=[[-1, P]], channel_multiplier=1).then_inc(s_const, 1)
            pool.dma_start(wq_nat[:], Wq_w).then_inc(s_small[4], 16)
            for k in range(NN):
                pool.dma_start(cw_nat[k * CO:(k + 1) * CO, :], cond_w).then_inc(s_small[0], 16)
            pool.wait_ge(s_cut, 1)
            for k in range(BY_SP, NG):
                relay(pool, k % NN, k // NN, s_blk0[k])
            pool.wait_ge(s_pads, 2)

            def cut(t):
                if isinstance(t, int):
                    pool.wait_ge(s_x0[t], 16)
                else:
                    pool.wait_ge(s_x, 16 * (t - 3))
                pool.wait_ge(s_blk, 16 * NG * (t - 1))
                nc.gpsimd.tensor_copy(x_cut[:], by_phase(t)).then_inc(s_cut, 1)

            cut(2)
            cut(3)
            with pool.Fori(4, NT) as t:
                cut(t)

        @block.scalar
        def _(act):
            def high(dst, src, s, scale=1.0):
                nc.scalar.activation(dst, src, ACT.Copy, scale=scale).then_inc(s, 1)

            def split_x(t):
                act.wait_ge(s_blk, 16 * NG * t)
                act.wait_ge(s_conv, 2 * t)
                high(x_hi[:], x_blk[:], s_xhi)

            def copy_h_bank(t, k):
                act.wait_ge(s_conv, 2 * t + k + 1)
                high(h_sb[:, k * G // 2:(k + 1) * G // 2], p_conv[:, k, :].rearrange("k (g n b) -> k g n b", n=NN, b=NB), s_hc)

            def copy_h(t):
                for k in range(2):
                    copy_h_bank(t, k)

            def split_h(t, k):
                act.wait_ge(s_ht, 2 * t + k + 1)
                for src, dst in h_views(t, k, h_hi):
                    last = nc.scalar.activation(dst, src, ACT.Copy)
                last.then_inc(s_hhi, 1)

            def split_z(t):
                act.wait_ge(s_ztp, t + 1)
                if not (isinstance(t, int) and t == NT - 1):
                    after(act, s_out, 2 * t)
                high(zt(t)[0], p_t[:].rearrange("j (c t) -> j c t", c=JC), s_zthi)

            def copy_q(i):
                act.wait_ge(s_qtp, i + 1)
                nc.scalar.activation(q_t[:], p_z[0:RD, 1, QT], ACT.Copy).then_inc(s_qt, 1)

            def exp(i):
                act.wait_ge(s_nm, i + 1)
                nc.scalar.activation(e_all[:], sc[:], ACT.Exp, bias=neg_max[:]).then_inc(s_e, 1)

            def body(i):
                if isinstance(i, int) and i == 1:
                    b_high(5)
                elif real(i - 1):
                    split_z(i - 1)
                if real(i):
                    copy_q(i)
                    if isinstance(i, int) and i == 1:
                        b_high(6)
                        split_z(0)
                        b_high(7)
                    exp(i)
                if real(i + 1):
                    copy_h(i + 1)
                    split_h(i + 1, 0)
                    split_h(i + 1, 1)
                if real(i + 2):
                    split_x(i + 2)

            def b_high(n):
                act.wait_ge(s_bt, n + 1)
                high(b_hi[:, n // 2, n % 2 * 512:(n % 2 + 1) * 512], p_out[:, n % 2, :], s_bhi, SCALING)

            def a_high(r):
                act.wait_ge(s_at, r + 1)
                high(a_hi[:, r, 0:J], a_bank(r), s_ahi)

            for k in range(NN):
                act.dma_start(bias2[k * CO:(k + 1) * CO, :], bias.rearrange("(o a) -> o a", a=1)).then_inc(s_small[1], 16)
            act.wait_ge(s_w, 16)
            for s in range(2):
                for r in range(W_DVE[s], R):
                    dst, src = w_shift(s, r)
                    high(dst, src, s_wc[s])
            for s in range(2):
                act.wait_ge(s_wt, s + 1)
                high(w_hi[:, s].rearrange("k g (r c) -> k r g c", c=CI),
                     p_out[:, s, :].rearrange("k (r g c) -> k r g c", g=G, c=CI), s_whi)

            def row_sums(c):
                act.wait_ge(s_a[c], 16)
                nc.scalar.activation(b_hi[:, c, :], a_nat[:, c, :], ACT.Copy, accum_out=row_sum[:, c:c + 1]).then_inc(s_rs[c], 1)

            for g in range(G):
                for n in range(NN):
                    act.wait_ge(s_blk0[g * NN + n], 16)
                high(x_hi[:, g * NN:(g + 1) * NN], x_blk[:, g * NN:(g + 1) * NN], s_xhi)
            act.wait_ge(s_st, 4)
            nc.scalar.activation(cw_t[:], p_t[:, CWT], ACT.Copy).then_inc(s_sc, 1)
            nc.scalar.activation(c_t[:], p_t[:, CT], ACT.Copy).then_inc(s_sc, 1)
            nc.scalar.activation(keys_t[:], p_t[0:RD, KT], ACT.Copy).then_inc(s_sc, 1)
            high(a_hi[:, :, J:JQ], p_t[:, WQT].rearrange("b (r q) -> b r q", q=RD), s_wqhi)
            copy_h(0)
            split_h(0, 0)
            split_h(0, 1)
            for r in range(R):
                a_high(r)
                if 1 <= r <= 3:
                    row_sums(r)
            b_high(0)
            split_x(1)
            b_high(1)
            act.wait_ge(s_bcp, 1)
            nc.scalar.activation(sum_bc[:, 0:J], p_conv[:, 0, :], ACT.Copy).then_inc(s_bc, 1)
            nc.scalar.activation(sum_bc[:, J:JQ], p_conv[:, 1, 0:RD], ACT.Copy).then_inc(s_bc, 1)
            b_high(2)
            copy_q(0)
            copy_h(1)
            split_h(1, 0)
            split_h(1, 1)
            b_high(3)
            b_high(4)
            exp(0)
            split_x(2)
            body(1)
            with act.Fori(2, NT - 2) as i:
                body(i)
            for i in range(NT - 2, NT + 1):
                body(i)

        @block.tensor
        def _(pe):
            def three(dst, s_hi, s_lo, m_hi, m_lo, first, last):
                nc.tensor.matmul(dst, s_hi, m_hi, start=first, stop=False)
                nc.tensor.matmul(dst, s_hi, m_lo, start=False, stop=False)
                return nc.tensor.matmul(dst, s_lo, m_hi, start=False, stop=last)

            def conv_group(g):
                k, at = g * 2 // G, g % (G // 2) * NN * NB
                for s in range(2):
                    blocks = (slice(None), slice(g * NN, (g + 1) * NN), slice(s, s + NB))
                    mm = three(p_conv[:, k, at:at + NN * NB], w_hi[:, s, g, :], w_lo[:, s, g, :],
                               x_hi[blocks], x_lo[blocks], s == 0, s == 1)
                if g % (G // 2) == G // 2 - 1:
                    mm.then_inc(s_conv, 1)

            def conv(t):
                pe.wait_ge(s_xhi, splits(t))
                pe.wait_ge(s_xlo, splits(t))
                for g in range(G):
                    conv_group(g)

            def turn_h(t, k):
                if early(t):
                    pe.wait_ge(s_hc, 2 * t + k + 1)
                    if k == 1:
                        after(pe, s_zs, 2 * t)
                    bank = (p_h[:], p_z[:, 0, :])[k]
                    pairs = [(n, g) for n in range(NN) for g in (2 * k, 2 * k + 1)]
                else:
                    if k == 0:
                        pe.wait_ge(s_hc, 2 * (t + 1))
                    else:
                        pe.wait_ge(s_hhi, 2 * t + 1)
                        pe.wait_ge(s_hlo, 2 * t + 1)
                    bank = p_h[:]
                    pairs = [(k, g) for g in range(G)]
                for at, (n, g) in enumerate(pairs):
                    mm = nc.tensor.transpose(bank[:, at * P:(at + 1) * P], h_sb[:, g, n, :], ident[:])
                mm.then_inc(s_ht, 1)

            def z_bank(k, phases):
                for r in phases:
                    cols = slice(k * HB, (k + 1) * HB)
                    mm = three(p_z[:, k, 0:HB], h_hi[:, r, :], h_lo[:, r, :], a_hi[:, r, cols], a_lo[:, r, cols],
                               r == 0, r == R - 1)
                return mm

            def turn_q(i):
                pe.wait_ge(s_q, i + 1)
                pe.wait_ge(s_zs, 2 * i + 1)
                nc.tensor.transpose(p_z[0:RD, 1, QT], q_s[:], ident[:]).then_inc(s_qtp, 1)

            def scores(i):
                pe.wait_ge(s_qt, i + 1)
                nc.tensor.matmul(p_z[:, 1, SC], q_t[:], keys_t[:], start=True, stop=True).then_inc(s_scp, 1)

            def turn_z(t):
                pe.wait_ge(s_zg, t + 1)
                for c in range(JC):
                    mm = nc.tensor.transpose(p_t[:, c * P:(c + 1) * P], z_g[:, c * P:(c + 1) * P], ident[:])
                mm.then_inc(s_ztp, 1)

            def out_part(t, k, chunks):
                if chunks[0] == 0 and k < 2:
                    after(pe, s_added, 2 * t + k - 1)
                dst, start, stop = parts(t)[k]
                cols = slice(start, stop)
                hi, lo = zt(t)
                for c in chunks:
                    mm = three(dst, hi[:, c, :], lo[:, c, :], b_hi[:, c, cols], b_lo[:, c, cols],
                               c == 0, c == JC - 1)
                if c == JC - 1:
                    mm.then_inc(s_out, 1)

            def body(i):
                if isinstance(i, int) and i == 1:
                    pe.wait_ge(s_dve, 1)
                elif real(i - 1) and real(i):
                    turn_z(i - 1)
                if real(i):
                    pe.wait_ge(s_hhi, 2 * (i + 1))
                    pe.wait_ge(s_hlo, 2 * (i + 1))
                    z_bank(1, range(R)).then_inc(s_zq, 1)
                    if isinstance(i, int) and i == 1:
                        turn_b(5)
                    z_bank(0, range(R // 2))
                    turn_q(i)
                    z_bank(0, range(R // 2, R)).then_inc(s_z, 1)
                    if isinstance(i, int) and i == 1:
                        turn_b(6)
                    scores(i)
                    if isinstance(i, int) and i == 1:
                        turn_z(0)
                        turn_b(7)
                if real(i + 1):
                    conv(i + 1)
                if isinstance(i, int) and i == 1:
                    pe.wait_ge(s_bhi, 2 * JC)
                    pe.wait_ge(s_blo, 2 * JC)
                if real(i - 1):
                    pe.wait_ge(s_zthi, i)
                    pe.wait_ge(s_ztlo, i)
                    out_part(i - 1, 0, range(JC // 2))
                if real(i + 1):
                    turn_h(i + 1, 0)
                if real(i - 1):
                    out_part(i - 1, 0, range(JC // 2, JC))
                    out_part(i - 1, 1, range(1))
                if real(i + 1):
                    turn_h(i + 1, 1)
                if isinstance(i, int) and i == NT - 1:
                    turn_z(i)
                    out_part(i - 1, 1, range(1, JC))
                elif real(i - 1):
                    out_part(i - 1, 1, range(1, JC))
                if isinstance(i, int) and i == NT:
                    out_part(i - 1, 2, range(JC))

            def turn_a(r):
                if r >= 3:
                    pe.wait_ge(s_ahi, r - 2)
                    pe.wait_ge(s_alo, r - 2)
                for c in range(JC):
                    if r == 0:
                        pe.wait_ge(s_a[c], 16)
                    mm = nc.tensor.transpose(a_bank(r)[:, c * P:(c + 1) * P],
                                             a_nat[:, c, :].rearrange("j (b r) -> j r b", r=R)[:, r, :], ident[:])
                mm.then_inc(s_at, 1)

            def turn_b(n):
                if n < 2:
                    pe.wait_ge(s_ahi, R - 1 + n)
                    pe.wait_ge(s_alo, R - 1 + n)
                else:
                    pe.wait_ge(s_bhi, n - 1)
                    pe.wait_ge(s_blo, n - 1)
                for c in range(4):
                    o = 4 * (n % 2) + c
                    if n < 2 and c % 2 == 0:
                        pe.wait_ge(s_b[o // 2], 16)
                    mm = nc.tensor.transpose(p_out[:, n % 2, c * P:(c + 1) * P],
                                             b_nat[:, o // 2, o % 2 * J + n // 2 * P:o % 2 * J + (n // 2 + 1) * P],
                                             ident[:])
                mm.then_inc(s_bt, 1)

            def warm(count):
                for _ in range(count):
                    nc.tensor.matmul(p_h[:, 0:P], ones[:], ones[:], start=True, stop=True)

            pe.wait_ge(s_const, 1)
            warm(WARM[0])
            pe.wait_ge(s_const, 2)
            for s in range(2):
                pe.wait_ge(s_wc[s], R)
                for r in range(R):
                    mm = nc.tensor.transpose(p_out[:, s, r * CO:(r + 1) * CO], w_cut[:, s, r, :], ident[0:CO, 0:CO])
                mm.then_inc(s_wt, 1)
            pe.wait_ge(s_small[4], 16)
            for r in range(R):
                mm = nc.tensor.transpose(p_t[:, WQT.start + r * RD:WQT.start + (r + 1) * RD],
                                         wq_nat[:].rearrange("q (b r) -> q r b", r=R)[:, r, :], ident[0:RD, 0:RD])
            mm.then_inc(s_st, 1)
            pe.wait_ge(s_small[0], 32)
            nc.tensor.transpose(p_t[:, CWT], cw_nat[:], ident[:]).then_inc(s_st, 1)
            warm(WARM[1])
            pe.wait_ge(s_small[2], 16)
            nc.tensor.transpose(p_t[:, CT], c_nat[:], ident[0:N, 0:N]).then_inc(s_st, 1)
            pe.wait_ge(s_small[3], 16)
            nc.tensor.transpose(p_t[0:RD, KT], keys_nat[:], ident[0:E, 0:E]).then_inc(s_st, 1)
            pe.wait_ge(s_whi, 2)
            pe.wait_ge(s_wlo, 2)
            for g in range(G):
                pe.wait_ge(s_xhi, g + 1)
                pe.wait_ge(s_xlo, g + 1)
                conv_group(g)
            pe.wait_ge(s_sc, 3)
            pe.wait_ge(s_wqlo, 1)
            nc.tensor.matmul(p_t[:, U], cw_t[:], c_t[:], start=True, stop=True).then_inc(s_up, 1)
            turn_h(0, 0)
            turn_h(0, 1)
            turn_a(0)
            turn_a(1)
            pe.wait_ge(s_u, NN)
            turn_a(2)
            pe.wait_ge(s_hhi, 2)
            pe.wait_ge(s_hlo, 2)
            for r in range(R):
                pe.wait_ge(s_ahi, r + 1)
                pe.wait_ge(s_alo, r + 1)
                z1 = z_bank(1, [r])
                z0 = z_bank(0, [r])
                if r + 3 < R:
                    turn_a(r + 3)
                else:
                    turn_b(r + 3 - R)
                if r == R - 2:
                    for c in range(JC + 1):
                        pe.wait_ge(s_dg, c + 1)
                        rows = P if c < JC else RD
                        dst = p_conv[:, 0, c * P:(c + 1) * P] if c < JC else p_conv[:, 1, 0:RD]
                        mm = nc.tensor.matmul(dst, ones[0:rows, :], diag[0:rows, c * P:c * P + rows], start=True, stop=True)
                    mm.then_inc(s_bcp, 1)
            z1.then_inc(s_zq, 1)
            z0.then_inc(s_z, 1)
            pe.wait_ge(s_xhi, splits(1))
            pe.wait_ge(s_xlo, splits(1))
            pe.wait_ge(s_bc, 2)
            conv_group(0)
            conv_group(1)
            turn_q(0)
            conv_group(2)
            conv_group(3)
            turn_h(1, 0)
            turn_b(3)
            turn_h(1, 1)
            scores(0)
            turn_b(4)
            body(1)
            with pe.Fori(2, NT - 1) as i:
                body(i)
            body(NT - 1)
            body(NT)

        @block.vector
        def _(dve):
            def low(dst, src, hi, s):
                nc.vector.tensor_tensor(dst, src, hi.bitcast(F32), ALU.subtract).then_inc(s, 1)

            def cut(t):
                dve.wait_ge(s_x0[t], 16)
                nc.vector.tensor_copy(x_cut[:], by_phase(t)).then_inc(s_cut, 1)

            def split_x(t):
                dve.wait_ge(s_xhi, splits(t))
                low(x_lo[:], x_blk[:], x_hi[:], s_xlo)

            def split_h(t, k):
                dve.wait_ge(s_hhi, 2 * t + k + 1)
                for src, dst, hi in h_views(t, k, h_lo, h_hi):
                    last = nc.vector.tensor_tensor(dst, src, hi.bitcast(F32), ALU.subtract)
                last.then_inc(s_hlo, 1)

            def split_z(t):
                dve.wait_ge(s_zthi, t + 1)
                low(zt(t)[1], p_t[:].rearrange("j (c t) -> j c t", c=JC), zt(t)[0], s_ztlo)

            STEPS = 7

            def copy_scores(i):
                dve.wait_ge(s_scp, i + 1)
                nc.vector.tensor_copy(sc[:], p_z[:, 1, SC]).then_inc(s_dve, 1)

            def gate(i):
                def step(n):
                    dve.wait_ge(s_dve, STEPS * i + n)

                def step_alone(n):
                    step(n)
                    dve.sem_inc(s_alone, 1)

                step_alone(1)
                nc.vector.max(top_a[:], sc[:]).then_inc(s_dve, 1)
                step(2)
                nc.vector.tensor_scalar(neg_max[:], top_a[:, 0:1], -1.0, None, ALU.mult).then_inc(s_nm, 1)
                nc.vector.match_replace(sc_a[:], top_a[:], sc[:], TAKEN).then_inc(s_dve, 1)
                step_alone(3)
                nc.vector.max(top_b[:], sc_a[:]).then_inc(s_dve, 1)
                step_alone(4)
                nc.vector.match_replace(sc_b[:], top_b[:], sc_a[:], TAKEN).then_inc(s_dve, 1)
                step(5)
                dve.wait_ge(s_e, i + 1)
                nc.vector.scalar_tensor_tensor(out=e_top[:], in0=sc_b[:], scalar=TAKEN, in1=e_all[:],
                                               op0=ALU.is_equal, op1=ALU.mult, accum_out=e_sum[:]).then_inc(s_dve, 1)
                step(6)
                nc.vector.reciprocal(e_inv[:], e_sum[:]).then_inc(s_dve, 1)
                step(7)
                dve.wait_ge(s_zs, 2 * (i + 1))
                nc.vector.scalar_tensor_tensor(
                    out=z_g[:].rearrange("t (e k) -> t e k", k=RANK),
                    in0=z_s[:].rearrange("t (e k) -> t e k", k=RANK), scalar=e_inv[:, 0:1],
                    in1=e_top[:].unsqueeze(2).to_broadcast([P, E, RANK]), op0=ALU.mult, op1=ALU.mult).then_inc(s_zg, 1)

            def add_u(i, dst, cols, src, s):
                nc.vector.scalar_tensor_tensor(out=dst, in0=sum_bc[:, cols], scalar=u[:, bass.ds(i, 1)], in1=src,
                                               op0=ALU.mult, op1=ALU.add).then_inc(s, 1)

            def z_out(i):
                dve.wait_ge(s_zq, i + 1)
                add_u(i, q_s[:], slice(J, JQ), p_z[:, 1, J - HB:HB], s_q)
                after(dve, s_zg, i)
                add_u(i, z_s[:, HB:J], slice(HB, J), p_z[:, 1, 0:J - HB], s_zs)
                if isinstance(i, int) and i == 1:
                    b_low(5)
                    split_x(2)
                dve.wait_ge(s_z, i + 1)
                add_u(i, z_s[:, 0:HB], slice(0, HB), p_z[:, 0, 0:HB], s_zs)

            def body(i):
                if real(i - 1) and real(i) and not (isinstance(i, int) and i == 1):
                    split_z(i - 1)
                if real(i):
                    z_out(i)
                    if isinstance(i, int) and i == 1:
                        b_low(6)
                    copy_scores(i)
                    if isinstance(i, int) and i == 1:
                        split_z(0)
                        b_low(7)
                    gate(i)
                if real(i + 1):
                    split_h(i + 1, 0)
                    split_h(i + 1, 1)
                if real(i - 1):
                    for k, (src, lo, hi) in enumerate(parts(i - 1)):
                        if k == 1 and real(i + 2):
                            split_x(i + 2)
                        if k == 1 and isinstance(i, int) and i == NT - 1:
                            split_z(i)
                        dve.wait_ge(s_out, 2 * (i - 1) + k + 1)
                        nc.vector.tensor_tensor(tile_cols(i - 1, lo, hi), src, tile_cols(i - 1, lo, hi),
                                                ALU.add).then_inc(s_added, 1)

            def b_low(n):
                dve.wait_ge(s_bhi, n + 1)
                cols = slice(n % 2 * 512, (n % 2 + 1) * 512)
                nc.vector.scalar_tensor_tensor(out=b_lo[:, n // 2, cols], in0=p_out[:, n % 2, :], scalar=SCALING,
                                               in1=b_hi[:, n // 2, cols].bitcast(F32), op0=ALU.mult,
                                               op1=ALU.subtract).then_inc(s_blo, 1)

            def row_sums(rows, src, landed, c):
                dve.wait_ge(landed, 16)
                nc.vector.tensor_reduce(row_sum[0:rows, c:c + 1], src, mybir.AxisListType.X, ALU.add).then_inc(s_rs[c], 1)

            def a_low(r):
                dve.wait_ge(s_ahi, r + 1)
                low(a_lo[:, r, 0:J], a_bank(r), a_hi[:, r, 0:J], s_alo)

            nc.vector.memset(w_pad[:], 0.0).then_inc(s_wz, 1)
            nc.vector.memset(x_all[:, :, 0:PAD], 0.0).then_inc(s_pads, 1)
            nc.vector.memset(x_all[:, :, PAD + L:LP], 0.0).then_inc(s_pads, 1)
            dve.wait_ge(s_pads, 2)
            cut(0)
            dve.wait_ge(s_w, 16)
            for s in range(2):
                for r in range(W_DVE[s]):
                    dst, src = w_shift(s, r)
                    nc.vector.tensor_copy(dst, src).then_inc(s_wc[s], 1)
            for s in range(2):
                dve.wait_ge(s_whi, s + 1)
                low(w_lo[:, s].rearrange("k g (r c) -> k r g c", c=CI),
                    p_out[:, s, :].rearrange("k (r g c) -> k r g c", g=G, c=CI),
                    w_hi[:, s].rearrange("k g (r c) -> k r g c", c=CI), s_wlo)
            for g in range(G):
                dve.wait_ge(s_xhi, g + 1)
                at = slice(g * NN, (g + 1) * NN)
                low(x_lo[:, at], x_blk[:, at], x_hi[:, at], s_xlo)
            row_sums(RD, wq_nat[:], s_small[4], JC)
            dve.wait_ge(s_wqhi, 1)
            low(a_lo[:, :, J:JQ], p_t[:, WQT].rearrange("b (r q) -> b r q", q=RD), a_hi[:, :, J:JQ], s_wqlo)
            row_sums(P, a_nat[:, 0, :], s_a[0], 0)

            def diagonal(c):
                rows = P if c < JC else RD
                dve.wait_ge(s_rs[c], 1)
                nc.vector.tensor_scalar(diag[0:rows, c * P:c * P + rows], ident[0:rows, 0:rows],
                                        row_sum[0:rows, c:c + 1], None, ALU.mult).then_inc(s_dg, 1)

            dve.wait_ge(s_up, 1)
            dve.wait_ge(s_small[1], 32)
            for k in range(NN):
                rows = slice(k * CO, (k + 1) * CO)
                nc.vector.tensor_scalar(u[rows, :], p_t[rows, U].rearrange("c (i n) -> c n i", n=NN)[:, k, :],
                                        bias2[rows, 0:1], None, ALU.add).then_inc(s_u, 1)
            split_h(0, 0)
            split_h(0, 1)
            dve.wait_ge(s_const, 2)
            for r in range(R):
                a_low(r)
                if r == 0:
                    cut(1)
                if 2 <= r <= JC + 2:
                    diagonal(r - 2)
            b_low(0)
            split_x(1)
            b_low(1)
            dve.wait_ge(s_bc, 2)
            dve.wait_ge(s_u, NN)
            z_out(0)
            b_low(2)
            split_h(1, 0)
            split_h(1, 1)
            copy_scores(0)
            b_low(3)
            b_low(4)
            gate(0)
            body(1)
            with dve.Fori(2, NT - 2) as i:
                body(i)
            for i in range(NT - 2, NT + 1):
                body(i)


_INS = ["x", "cond_128", "fside_S_0", "L0_cond_weight", "L0_cond_c_weight", "L0_ffn_A_w", "L0_ffn_B_w",
        "L0_ffn_Wq_w", "L0_ffn_keys"]


def kernel(**inputs):
    import numpy as np
    import concourse.bacc as bacc
    from concourse.bass_utils import run_bass_kernel_spmd

    nc = bacc.Bacc("TRN2", target_bir_lowering=False, num_devices=1)
    arrays, args = {}, []
    for name in _INS:
        a = np.ascontiguousarray(inputs[name])
        arrays[f"in_{name}"] = a
        args.append(nc.dram_tensor(f"in_{name}", a.shape, mybir.dt.from_np(a.dtype), kind="ExternalInput").ap())
    shape = inputs["x"].shape
    args.append(nc.dram_tensor("out_dram", shape, F32, kind="ExternalOutput").ap())
    adaln_ffn(nc, *args)
    r = run_bass_kernel_spmd(nc, [arrays], core_ids=[0])
    return r.results[0]["out_dram"]
```
